# Optimizing a Trainium2 kernel written in Bass

```python
import numpy as np
import jax
import jax.numpy as jnp

def _softmax(x, axis=-1):
    return jax.nn.softmax(x, axis=axis)

def _gelu(x):
    return jax.nn.gelu(x, approximate=True)

def _silu(x):
    return jax.nn.silu(x)

def _sigmoid(x):
    return jax.nn.sigmoid(x)

def _layernorm(x, axis=-1, eps=1e-05):
    m = jnp.mean(x, axis=axis, keepdims=True)
    v = jnp.var(x, axis=axis, keepdims=True)
    return (x - m) / jnp.sqrt(v + eps)

def _scatter_add(tgt, idx, src, axis=0):
    return tgt.at[idx].add(src)

def _segment_sum(src, seg, n):
    return jax.ops.segment_sum(src, seg, n)
kernel_name = 'mk_decoder_preln_d1_seqx_r8_5a46d4'

def setup_inputs(seed: int=0):
    np.random.seed(seed)
    _w = jnp.asarray

    def _rec_inputs():
        import jax
        import jax.numpy as jnp
        _rk = jax.random.key(seed)
        x = 0.0002417 + 0.9998 * jax.random.normal(jax.random.fold_in(_rk, 1), (32, 128, 128), jnp.float32)
        _lenS = 128 - jax.random.randint(jax.random.fold_in(_rk, 7), (32,), 0, max(1, 128 // 4) + 1, jnp.int32)
        _lenS2 = 128 - jax.random.randint(jax.random.fold_in(_rk, 8), (32,), 0, max(1, 128 // 4) + 1, jnp.int32)
        _ctx_1024P = jax.random.normal(jax.random.fold_in(_rk, 11), (32, 16, 128), jnp.float32)
        _ctx_1024c = jax.random.dirichlet(jax.random.fold_in(_rk, 511), 0.3 * jnp.ones((16,), jnp.float32), (32, 128))
        _ctx_1024t = jnp.einsum('bsk,bkd->bsd', _ctx_1024c, _ctx_1024P)
        _ctx_1024t = _ctx_1024t * jax.lax.rsqrt(jnp.mean(jnp.square(_ctx_1024t)) + 1e-12) * 0.953939
        ctx_1024 = 7.22013e-05 + 1.00017 * (_ctx_1024t + 0.3 * jax.random.normal(jax.random.fold_in(_rk, 611), (32, 128, 128), jnp.float32))
        return (x, ctx_1024)
    x, ctx_1024 = _rec_inputs()

    def _L0_attn_setup():
        import jax, jax.numpy as jnp
        import numpy as np
        import math
        B, T, C = (2, 256, 128)
        NH = 16
        HD = C // NH

        def _rope_factor(T, d, dtype):
            theta = 1.0 / 10000.0 ** (2.0 * jnp.arange(0, d // 2, dtype=jnp.float32) / d)
            seq = jnp.arange(1, T + 1, dtype=jnp.float32)
            ang = jnp.einsum('n,d->nd', seq, theta)
            ang = jnp.concatenate([ang, ang], axis=-1)
            return (jnp.cos(ang) + jnp.sin(ang)).astype(dtype)
        key = jax.random.key(seed)
        ks = jax.random.split(key, 5)
        s = 0.02
        return {'x': jax.random.normal(ks[0], (B, T, C), dtype=jnp.float32), 'W_attn': jax.random.normal(ks[1], (3 * C, C), dtype=jnp.float32) * s, 'b_attn': jax.random.normal(ks[2], (3 * C,), dtype=jnp.float32) * s, 'W_proj': jax.random.normal(ks[3], (C, C), dtype=jnp.float32) * s, 'b_proj': jax.random.normal(ks[4], (C,), dtype=jnp.float32) * s}
    _L0_attn_all = _L0_attn_setup()
    _L0_attn_in = {k: v for k, v in _L0_attn_all.items() if k in ('W_attn', 'b_attn', 'W_proj', 'b_proj')}
    del _L0_attn_all

    def _L0_xattn_setup():
        import jax, jax.numpy as jnp
        import numpy as np
        D_MODEL = 128
        B, S = (4, 256)
        key = jax.random.key(seed)
        ks = jax.random.split(key, 10)
        s = 1.0 / np.sqrt(D_MODEL)
        return {'k': jax.random.normal(ks[0], (B, S, D_MODEL), jnp.float32), 'v': jax.random.normal(ks[1], (B, S, D_MODEL), jnp.float32), 'q': jax.random.normal(ks[2], (B, S, D_MODEL), jnp.float32), 'Wk': jax.random.normal(ks[3], (D_MODEL, D_MODEL), jnp.float32) * s, 'Wv': jax.random.normal(ks[4], (D_MODEL, D_MODEL), jnp.float32) * s, 'bv': jnp.zeros((D_MODEL,), jnp.float32), 'Wq': jax.random.normal(ks[5], (D_MODEL, D_MODEL), jnp.float32) * s, 'bq': jnp.zeros((D_MODEL,), jnp.float32), 'Wo': jax.random.normal(ks[6], (D_MODEL, D_MODEL), jnp.float32) * s, 'bo': jnp.zeros((D_MODEL,), jnp.float32)}
    _L0_xattn_all = _L0_xattn_setup()
    _L0_xattn_in = {k: v for k, v in _L0_xattn_all.items() if k in ('Wk', 'Wv', 'bv', 'Wq', 'bq', 'Wo', 'bo')}
    del _L0_xattn_all

    def _L0_ffn_setup():
        import jax, jax.numpy as jnp
        import numpy as np
        B, S, D, F, E, K = (4, 256, 128, 256, 8, 2)
        key = jax.random.key(seed)
        ks = jax.random.split(key, 9)
        sc = 0.02
        return {'hidden_states': jax.random.normal(ks[0], (B, S, D), jnp.float32), 'router_w': jax.random.normal(ks[1], (E, D), jnp.float32) * sc, 'w_gate': jax.random.normal(ks[2], (E, D, F), jnp.float32) * sc, 'w_up': jax.random.normal(ks[3], (E, D, F), jnp.float32) * sc, 'w_down': jax.random.normal(ks[4], (E, F, D), jnp.float32) * sc, 'sw_gate': jax.random.normal(ks[5], (D, F), jnp.float32) * sc, 'sw_up': jax.random.normal(ks[6], (D, F), jnp.float32) * sc, 'sw_down': jax.random.normal(ks[7], (F, D), jnp.float32) * sc, 'gate_w': jax.random.normal(ks[8], (1, D), jnp.float32) * sc}
    _L0_ffn_all = _L0_ffn_setup()
    _L0_ffn_in = {k: v for k, v in _L0_ffn_all.items() if k in ('router_w', 'w_gate', 'w_up', 'w_down', 'sw_gate', 'sw_up', 'sw_down', 'gate_w')}
    del _L0_ffn_all
    return {'x': x, 'ctx_1024': ctx_1024, 'L0_attn_W_attn': _L0_attn_in['W_attn'], 'L0_attn_b_attn': _L0_attn_in['b_attn'], 'L0_attn_W_proj': _L0_attn_in['W_proj'], 'L0_attn_b_proj': _L0_attn_in['b_proj'], 'L0_xattn_Wk': _L0_xattn_in['Wk'], 'L0_xattn_Wv': _L0_xattn_in['Wv'], 'L0_xattn_bv': _L0_xattn_in['bv'], 'L0_xattn_Wq': _L0_xattn_in['Wq'], 'L0_xattn_bq': _L0_xattn_in['bq'], 'L0_xattn_Wo': _L0_xattn_in['Wo'], 'L0_xattn_bo': _L0_xattn_in['bo'], 'L0_ffn_router_w': _L0_ffn_in['router_w'], 'L0_ffn_w_gate': _L0_ffn_in['w_gate'], 'L0_ffn_w_up': _L0_ffn_in['w_up'], 'L0_ffn_w_down': _L0_ffn_in['w_down'], 'L0_ffn_sw_gate': _L0_ffn_in['sw_gate'], 'L0_ffn_sw_up': _L0_ffn_in['sw_up'], 'L0_ffn_sw_down': _L0_ffn_in['sw_down'], 'L0_ffn_gate_w': _L0_ffn_in['gate_w']}

def reference(x, ctx_1024, L0_attn_W_attn, L0_attn_b_attn, L0_attn_W_proj, L0_attn_b_proj, L0_xattn_Wk, L0_xattn_Wv, L0_xattn_bv, L0_xattn_Wq, L0_xattn_bq, L0_xattn_Wo, L0_xattn_bo, L0_ffn_router_w, L0_ffn_w_gate, L0_ffn_w_up, L0_ffn_w_down, L0_ffn_sw_gate, L0_ffn_sw_up, L0_ffn_sw_down, L0_ffn_gate_w):
    import jax
    import jax.numpy as jnp

    def _L0_attn_ref(x, W_attn, b_attn, W_proj, b_proj):
        import jax, jax.numpy as jnp
        import numpy as np
        import math
        B, T, C = (2, 256, 128)
        NH = 16
        HD = C // NH

        def _rope_factor(T, d, dtype):
            theta = 1.0 / 10000.0 ** (2.0 * jnp.arange(0, d // 2, dtype=jnp.float32) / d)
            seq = jnp.arange(1, T + 1, dtype=jnp.float32)
            ang = jnp.einsum('n,d->nd', seq, theta)
            ang = jnp.concatenate([ang, ang], axis=-1)
            return (jnp.cos(ang) + jnp.sin(ang)).astype(dtype)
        Bs, Ts, Cs = x.shape
        qkv = x @ W_attn.T + b_attn
        q, k, v = jnp.split(qkv, 3, axis=-1)

        def to_heads(t):
            return t.reshape(Bs, Ts, NH, HD).transpose(0, 2, 1, 3)
        q, k, v = (to_heads(q), to_heads(k), to_heads(v))
        f = _rope_factor(Ts, HD, x.dtype)
        q = q * f
        k = k * f
        att = jnp.einsum('bhqd,bhkd->bhqk', q, k) * (1.0 / math.sqrt(HD))
        causal = jnp.tril(jnp.ones((Ts, Ts), dtype=bool))
        att = jnp.where(causal, att, jnp.finfo(att.dtype).min)
        att = jax.nn.softmax(att, axis=-1)
        y = jnp.einsum('bhqk,bhkd->bhqd', att, v)
        y = y.transpose(0, 2, 1, 3).reshape(Bs, Ts, Cs)
        y = y @ W_proj.T + b_proj
        return y

    def _L0_xattn_ref(k, v, q, Wk, Wv, bv, Wq, bq, Wo, bo):
        import jax, jax.numpy as jnp
        import numpy as np
        D_MODEL = 128
        B, S = (4, 256)
        kp = jnp.einsum('bsd,ed->bse', k, Wk)
        vp = jnp.einsum('bsd,ed->bse', v, Wv) + bv
        qp = jnp.einsum('bsd,ed->bse', q, Wq) + bq
        scale = 1.0 / jnp.sqrt(jnp.float32(kp.shape[-1]))
        scores = jnp.einsum('bqd,bkd->bqk', qp, kp) * scale
        probs = jax.nn.softmax(scores, axis=-1)
        ctx = jnp.einsum('bqk,bkd->bqd', probs, vp)
        return jnp.einsum('bqd,ed->bqe', ctx, Wo) + bo

    def _L0_ffn_ref(hidden_states, router_w, w_gate, w_up, w_down, sw_gate, sw_up, sw_down, gate_w):
        import jax, jax.numpy as jnp
        import numpy as np
        B, S, D, F, E, K = (4, 256, 128, 256, 8, 2)
        bsz, seq_len, d = hidden_states.shape
        x = hidden_states.reshape(-1, d)
        T = x.shape[0]
        n_exp = router_w.shape[0]
        logits = x @ router_w.T
        probs = jax.nn.softmax(logits, axis=-1)
        rw, sel = jax.lax.top_k(probs, K)
        cw = jnp.zeros((T, n_exp), x.dtype).at[jnp.arange(T)[:, None], sel].set(rw)
        g = jnp.einsum('td,edf->etf', x, w_gate)
        u = jnp.einsum('td,edf->etf', x, w_up)
        h = jax.nn.silu(g) * u
        y = jnp.einsum('etf,efd->etd', h, w_down)
        moe_out = jnp.einsum('te,etd->td', cw, y)
        shared = jax.nn.silu(x @ sw_gate) * (x @ sw_up) @ sw_down
        gate = jax.nn.sigmoid(x @ gate_w.T)
        out = moe_out + gate * shared
        return out.reshape(bsz, seq_len, d)
    x = x + _L0_attn_ref(_layernorm(x, axis=-1), L0_attn_W_attn, L0_attn_b_attn, L0_attn_W_proj, L0_attn_b_proj)
    x = x + _L0_xattn_ref(ctx_1024, ctx_1024, _layernorm(x, axis=-1), L0_xattn_Wk, L0_xattn_Wv, L0_xattn_bv, L0_xattn_Wq, L0_xattn_bq, L0_xattn_Wo, L0_xattn_bo)
    x = x + _L0_ffn_ref(_layernorm(x, axis=-1), L0_ffn_router_w, L0_ffn_w_gate, L0_ffn_w_up, L0_ffn_w_down, L0_ffn_sw_gate, L0_ffn_sw_up, L0_ffn_sw_down, L0_ffn_gate_w)
    return x

_drawn_inputs = setup_inputs


def setup_inputs(seed=0):
    import zlib

    import numpy as np

    out = dict(_drawn_inputs(seed))
    spreads = {'L0_xattn_bv': (0.0, 0.1), 'L0_xattn_bq': (0.0, 0.338), 'L0_xattn_bo': (0.0, 0.1)}
    factors = {'L0_attn_W_attn': 5.984,
     'L0_attn_b_attn': 8.0,
     'L0_attn_W_proj': 5.41,
     'L0_attn_b_proj': 3.11,
     'L0_ffn_router_w': 8.0,
     'L0_ffn_w_gate': 8.0,
     'L0_ffn_w_up': 8.0,
     'L0_ffn_w_down': 8.0,
     'L0_ffn_sw_gate': 8.0,
     'L0_ffn_sw_up': 8.0,
     'L0_ffn_sw_down': 8.0,
     'L0_ffn_gate_w': 8.0}
    for name, (base, spread) in spreads.items():
        noise = np.random.default_rng([zlib.crc32(name.encode()), seed]).standard_normal(out[name].shape)
        drawn = base * np.exp(spread * noise) if base else spread * noise
        out[name] = jnp.asarray(drawn.astype(out[name].dtype))
    for name, factor in factors.items():
        out[name] = (out[name] * factor).astype(out[name].dtype)
    return out
```

```python
from contextlib import ExitStack

import concourse.bass as bass
from concourse import mybir

fp32 = mybir.dt.float32
fp32r = mybir.dt.float32r
bf16 = mybir.dt.bfloat16
ALU = mybir.AluOpType
ACT = mybir.ActivationFunctionType
AX = mybir.AxisListType

B = 32
T = 128
C = 128
NH = 16
HD = C // NH
GB = 4
NG = B // GB
HJ = 4
NJ = NH // HJ
QF = HJ * HD
KR = 3 * QF
VW = 32
E = 8
FF = 256
NE = E + 1
FT = FF // 128
EPS = 1e-5
QSCALE = HD ** -0.5
XSCALE = C ** -0.5
MASKED = -3.0e38

STEADY = (8, 28)
LAST_LAG = 6


def timeline(s):
    u, g = s % GB, s // GB
    ahead = g + 1 < NG
    out = []

    def batch(name, b, *more):
        if 0 <= b < B:
            out.append((name, b, *more))

    batch("scores", s, 0)
    if u != 3:
        batch("stacks", s + 1)
    elif ahead:
        out.append(("project", g + 1, 4))
    batch("turn_xprobs", s - 5)
    if u == 2 and ahead:
        out.append(("turn_x", g + 1))
    batch("scores_t", s - 1, 0)
    batch("turn_y", s - 3)
    if u == 3 and ahead:
        out.append(("project", g + 1, 5))
    batch("scores", s, 1)
    batch("xproject", s - 4)
    if u == 3 and ahead:
        out.append(("project", g + 1, 6))
    if u == 0 and ahead:
        out.append(("norm_x_stats", g + 1))
    if u == 1 and ahead:
        out.append(("norm_x", g + 1))
    batch("scores_t", s - 1, 1)
    batch("attn_out", s - 3)
    if u == 3 and ahead:
        out.append(("project", g + 1, 7))
    batch("scores", s, 2)
    batch("values", s - 2)
    batch("turn_ffn", s - 6)
    if u == 3:
        batch("stacks", s + 1)
    elif u == 2 and ahead:
        out.append(("project", g + 1, 0))
    batch("scores_t", s - 1, 2)
    batch("xout", s - 5)
    batch("norm_xattn", s - 3)
    if u == 2 and ahead:
        out.append(("project", g + 1, 1))
    batch("scores", s, 3)
    batch("xscores", s - 4)
    batch("project_v", s + 2)
    if u == 2 and ahead:
        out.append(("project", g + 1, 2))
    batch("scores_t", s - 1, 3)
    batch("tall_sums", s - 2)
    batch("router", s - 6)
    batch("turn_x2", s - 3)
    batch("norm_ffn", s - 5)
    if u == 2 and ahead:
        out.append(("project", g + 1, 3))
    return out


def prologue():
    return ([("norm_x_stats", 0), ("norm_x", 0), ("turn_x", 0)] + [("project", 0, n) for n in range(8)]
            + [("stacks", 0), ("project_v", 0), ("project_v", 1)])


SHARED = 4
CONSTS = 20
W_LOADS = 17
BANK = {"turn_xprobs": 0, "turn_y": 1, "xproject": 2, "attn_out": 3, "values": 0, "turn_ffn": 1,
        "xout": 2, "xscores": 3, "project_v": 0, "tall_sums": 1, "router": 2, "turn_x2": 3, "turn_x": 2,
        "project": (2, 3, 1, 0, 1, 2, 3, 0)}
SETUP_FILLS = (1, 1, 1, 1)


def bank_fills():
    count, fill = list(SETUP_FILLS), {}
    for item in prologue() + [x for s in range(B + LAST_LAG) for x in timeline(s)]:
        name = item[0]
        if name not in BANK:
            continue
        bank = BANK[name][item[2]] if name == "project" else BANK[name]
        fill[item] = (bank, count[bank])
        count[bank] += 1
    return fill, count


GROUP_STAGES = ("turn_x", "project")
FILL, FILLS = bank_fills()
PER_GROUP = [sum(1 for s in range(STEADY[0], STEADY[0] + GB) for x in timeline(s) if x in FILL and FILL[x][0] == k)
             for k in range(SHARED)]


def build(nc, x, ctx_in, W_attn, b_attn, W_proj, b_proj, Wk, Wv, bv, Wq, bq, Wo, bo, router_w,
          w_gate, w_up, w_down, sw_gate, sw_up, sw_down, gate_w, rope, out):
    ctx = ExitStack()
    with ctx:
        def sb(name, shape, dt=fp32):
            return ctx.enter_context(nc.sbuf_tensor(name, shape, dt))

        def sem(name):
            return ctx.enter_context(nc.semaphore(name))

        res = sb("res", [T, B, C])
        x3T = sb("x3T", [C, B * T])
        t_qk = sb("t_qk", [128, 2 * NJ, GB * T])
        qk_stack = sb("qk_stack", [KR, 4, 2 * NJ, T], fp32r)
        wide = sb("wide", [128, 2 * NE * 2 * FF], fp32r)
        q_slots = wide[0:KR, 0:4 * NJ * HJ * T].rearrange("p (r j i t) -> p r j i t", r=4, j=NJ, i=HJ)
        wgu_hi = wide[:, 0:NE * 2 * FF].rearrange("p (e f) -> p e f", e=NE)
        wgu_lo = wide[:, NE * 2 * FF:].rearrange("p (e f) -> p e f", e=NE)
        k_slots = sb("k_slots", [KR, 2, NJ, HJ, T], fp32r)
        negmax = sb("negmax", [T, 2, NH])
        dmax = sb("dmax", [T, NH, T], fp32r)
        probs = sb("probs", [T, 2, NH, T])
        vst = sb("vst", [T, GB, NH, VW])
        xn1 = sb("xn1", [T, GB, C])
        xT = sb("xT", [C, GB * T])
        xT_hi = sb("xT_hi", [C, 2, GB * T], fp32r)
        xT_lo = sb("xT_lo", [C, 2, GB * T], fp32r)
        yu = sb("yu", [T, NJ * T])
        ysum = sb("ysum", [T, NH])
        yn = sb("yn", [T, C])
        ynT = sb("ynT", [C, T])
        x1 = sb("x1", [T, 4, C])
        x1b = sb("x1b", [T, 4, C])
        xn2 = sb("xn2", [T, C])
        ctx_t = sb("ctx_t", [T, 4, C])
        xcT = sb("xcT", [C, 2, 2, T])
        qa = sb("qa", [C, T])
        cm = sb("cm", [T, 2, C])
        xneg = sb("xneg", [T, 1])
        xsum = sb("xsum", [T, 2, 1])
        xinv = sb("xinv", [T, 1])
        xprobs = sb("xprobs", [T, T])
        xprobsT = sb("xprobsT", [T, T])
        xn3 = sb("xn3", [T, C])
        x3s = sb("x3s", [C, T])
        st1 = sb("st1", [T, GB, 6]); mv1 = sb("mv1", [T, GB, 2]); ln1 = sb("ln1", [T, GB]); rs1 = sb("rs1", [T, GB])
        st2 = sb("st2", [T, 6]); mv2 = sb("mv2", [T, 2]); ln2 = sb("ln2", [T, 1]); rs2 = sb("rs2", [T, 1])
        st3 = sb("st3", [T, 6]); mv3 = sb("mv3", [T, 2]); ln3 = sb("ln3", [T, 1]); rs3 = sb("rs3", [T, 1])
        logit = sb("logit", [T, B, NE])

        ident = sb("ident", [128, 128])
        ident16 = sb("ident16", [128, 128], bf16)
        causal = sb("causal", [T, HJ, T], bf16)
        ones_r = sb("ones_r", [T, T], fp32r)
        slot_rows = sb("slot_rows", [KR, HJ])
        eps = sb("eps", [T, 1])
        ropes = sb("ropes", [KR, 2, T])
        bqk = sb("bqk", [KR, 2 * NJ])
        wr = sb("wr", [NE, C])
        cols = sb("cols", [C, 3])
        rows = sb("rows", [1, 2, C])
        one_row = sb("one_row", [1, 128])
        wqk_hi = sb("wqk_hi", [C, 2 * NJ, 3, QF], fp32r)
        wqk_lo = sb("wqk_lo", [C, 2 * NJ, 3, QF], fp32r)
        wvT = sb("wvT", [C, C]); wpT = sb("wpT", [C, C]); woT = sb("woT", [C, C])
        wrT = sb("wrT", [C, NE])
        wA = sb("wA", [C, C])
        wM = sb("wM", [C, C])
        bqA = sb("bqA", [C, 1])
        bias1 = sb("bias1", [T, C])
        bias2 = sb("bias2", [T, C])
        wd = sb("wd", [128, NE, FT, C])
        flat = probs[:].rearrange("p r h t -> p (r h t)")
        raw = flat[:, 0:12 * C].rearrange("p (k c) -> p k c", c=C)
        wa = raw[:, 0:3, :]
        wsq = raw[:, 3:8, :]
        bcol = raw[:, 8:10, :]
        wqkT = raw[:, 10:12, :]
        h_all = flat[:, 0:2 * FT * 512].rearrange("p (r f t) -> p r f t", r=2, f=FT)
        silu = flat[:, 2 * FT * 512:3 * FT * 512].rearrange("p (f t) -> p f t", f=FT)
        cw = sb("cw", [T, B, NE])
        top_p = sb("top_p", [T, B, 1]); gexp = sb("gexp", [T, B, 1])
        vflat = vst[:].rearrange("p u h v -> p (u h v)")
        ramp, sel1, sel2, pick, rest = (vflat[:, k * B * E:(k + 1) * B * E].rearrange("p (b e) -> p b e", b=B) for k in range(5))

        PS = [ctx.enter_context(nc.psum_tensor(f"ps_scores{i}", [T, 512], fp32)) for i in range(2)]
        PT = [ctx.enter_context(nc.psum_tensor(f"ps_scores_t{i}", [T, 512], fp32)) for i in range(2)]
        PM = [ctx.enter_context(nc.psum_tensor(f"ps_shared{i}", [T, 512], fp32)) for i in range(SHARED)]

        x_in = [sem("x_in0"), sem("x_in1")]
        w_in = sem("w_in"); wd_in = sem("wd_in"); wgu_in = sem("wgu_in")
        ctx_loaded = [sem(f"ctx_loaded{i}") for i in range(4)]
        out_written = sem("out_written")
        filled = [sem(f"bank_filled{i}") for i in range(SHARED)]
        drained = [sem(f"bank_drained{i}") for i in range(SHARED)]
        const_ready = sem("const_ready"); pool_step = sem("pool_step"); setup_done = sem("setup_done")
        dve_step = sem("dve_step"); act_step = sem("act_step")
        x_stats = sem("x_stats"); x_rstd = sem("x_rstd"); x_normed = sem("x_normed")
        x_part = sem("x_part"); x_ln = sem("x_ln"); xhi_done = sem("xhi_done"); xT_split = sem("xT_split")
        xbias_added = sem("xbias_added")
        rounded = sem("rounded"); stacked = sem("stacked"); q_slotted = sem("q_slotted"); k_slotted = sem("k_slotted")
        scored = sem("scored"); maxed = sem("maxed"); scored_t = sem("scored_t")
        exped = sem("exped"); probs_ready = sem("probs_ready")
        diag_ready = sem("diag_ready"); y_inverse = sem("y_inverse")
        x1_part = sem("x1_part"); x1_stats = sem("x1_stats"); x1_ln = sem("x1_ln"); x1_rstd = sem("x1_rstd")
        x1b_ready = sem("x1b_ready"); xn2_ready = sem("xn2_ready"); xneg_ready = sem("xneg_ready")
        x_inverse = sem("x_inverse")
        x2_part = sem("x2_part"); x2_stats = sem("x2_stats"); x2_ln = sem("x2_ln"); x2_rstd = sem("x2_rstd")
        xn3_ready = sem("xn3_ready"); x3T_kept = sem("x3T_kept")
        centred = sem("centred"); route_exped = sem("route_exped"); cw_ready = sem("cw_ready")
        wgu_split = sem("wgu_split")
        xb_split = sem("xb_split"); xb_hi_done = sem("xb_hi_done")
        gate_done = sem("gate_done"); up_done = sem("up_done"); silu_done = sem("silu_done"); h_ready = sem("h_ready")
        down_done = sem("down_done"); mixed = sem("mixed")

        block = ctx.enter_context(nc.Block())

        class Waits:

            def __init__(self, engine):
                self.engine, self.it = engine, None

            def count(self, n, per_group):
                return n if self.it is None else n + self.it * per_group

            def ge(self, s, n, rate=1):
                if n > 0:
                    self.engine.wait_ge(s, self.count(n, rate * GB))

            def ge_group(self, s, n, rate=1):
                if n > 0:
                    self.engine.wait_ge(s, self.count(n, rate))

            def alone(self):
                if self.it is not None:
                    self.engine.nop(nofuse=True)

            def batch(self, b):
                return b if self.it is None else b + self.it * GB

            def bank_free(self, item):
                bank, n = FILL[item]
                if n:
                    self.engine.wait_ge(drained[bank], self.count(n, PER_GROUP[bank]))
                return PM[bank]

            def bank_filled(self, item):
                bank, n = FILL[item]
                self.engine.wait_ge(filled[bank], self.count(n + 1, PER_GROUP[bank]))
                return PM[bank], drained[bank]

            def bank_read(self, item):
                name, b, *more = item
                if b < 0:
                    return
                bank, n = FILL[item]
                if self.it is not None:
                    step = 1 if name in GROUP_STAGES else GB
                    assert FILL[(name, b + step, *more)][1] - n == PER_GROUP[bank], item
                self.engine.wait_ge(drained[bank], self.count(n + 1, PER_GROUP[bank]))

            def run(self, stages):
                def take(items):
                    for name, *args in items:
                        if name in stages:
                            stages[name](*args)

                take(prologue())
                for s in range(STEADY[0]):
                    take(timeline(s))
                with self.engine.Fori(0, (STEADY[1] - STEADY[0]) // GB) as it:
                    self.it = it
                    for s in range(STEADY[0], STEADY[0] + GB):
                        take(timeline(s))
                self.it = None
                for s in range(STEADY[1], B + LAST_LAG):
                    take(timeline(s))

        def put_bank(item):
            return filled[FILL[item][0]]

        @block.sync
        def _(sp):
            w = Waits(sp)
            sp.dma_start(res[:, 0:GB, :], x[0:GB].rearrange("b t c -> t b c")).then_inc(x_in[0], 16)
            sp.dma_start(wa, W_attn.rearrange("(k p) c -> p k c", p=128)).then_inc(w_in, 16)
            for n, m in enumerate((W_proj, Wk, Wv, Wq, Wo)):
                sp.dma_start(wsq[:, n, :], m).then_inc(w_in, 16)
            sp.dma_start(wr[0:E, :], router_w).then_inc(w_in, 16)
            sp.dma_start(wr[E:NE, :], gate_w).then_inc(w_in, 16)
            sp.dma_start(cols[:, 0:1], b_attn[2 * C:3 * C].rearrange("(p a) -> p a", a=1)).then_inc(w_in, 16)
            sp.dma_start(cols[:, 1:2], bv.rearrange("(p a) -> p a", a=1)).then_inc(w_in, 16)
            sp.dma_start(cols[:, 2:3], bq.rearrange("(p a) -> p a", a=1)).then_inc(w_in, 16)
            sp.dma_start(rows[:, 0, :], b_proj.rearrange("(a n) -> a n", a=1)).then_inc(w_in, 16)
            sp.dma_start(rows[:, 1, :], bo.rearrange("(a n) -> a n", a=1)).then_inc(w_in, 16)
            for r in range(3):
                sp.dma_start(bqk[QF * r:QF * r + QF, :], b_attn[0:2 * C].rearrange("(j p) -> p j", p=QF),
                             allow_slow_non_contiguous=True).then_inc(w_in, 16)
            sp.dma_start(ropes[:], rope).then_inc(w_in, 16)
            sp.dma_start(res[:, GB:B, :], x[GB:B].rearrange("b t c -> t b c")).then_inc(x_in[1], 16)
            for u in range(4):
                sp.dma_start(ctx_t[:, u, :], ctx_in[u]).then_inc(ctx_loaded[u], 16)
            for e in range(NE):
                sp.dma_start(wd[:, e, :, :], (w_down[e] if e < E else sw_down).rearrange("(k p) c -> p k c", p=128))\
                    .then_inc(wd_in, 16)

            def turn_x2(b):
                if w.it is None and b + 4 >= B:
                    return
                w.bank_read(("turn_x2", b))
                sp.dma_start(ctx_t[:, b % 4, :], ctx_in[bass.ds(w.batch(b + 4), 1), :, :].rearrange("a t c -> t (a c)"))\
                    .then_inc(ctx_loaded[b % 4], 16)

            w.run(dict(turn_x2=turn_x2))
            sp.wait_ge(stacked, B)
            sp.wait_ge(rounded, B)
            w.bank_read(("project_v", B - 1))
            for e in range(NE):
                for k, m in enumerate((w_gate[e], w_up[e]) if e < E else (sw_gate, sw_up)):
                    dst = t_qk[:, e, :] if e < E else xT[:]
                    sp.dma_start(dst[:, k * FF:(k + 1) * FF], m).then_inc(wgu_in, 16)
            with sp.Fori(0, NG) as g:
                sp.wait_ge(mixed, g * NE + NE)
                sp.dma_start(out[bass.ds(g * GB, GB), :, :].rearrange("b t c -> t b c"),
                             res[:, bass.ds(g * GB, GB), :]).then_inc(out_written, 16)
            sp.wait_ge(out_written, 16 * NG)

        @block.gpsimd
        def _(pool):
            w = Waits(pool)
            steps = [0]

            def step(ins):
                steps[0] += 1
                ins.then_inc(pool_step, 1)
                pool.wait_ge(pool_step, steps[0])

            def const(ins):
                consts[0] += 1
                ins.then_inc(const_ready, 1)
                pool.wait_ge(const_ready, consts[0])

            consts = [0]
            for m in (ident, ident16):
                const(pool.memset(m[:], 0.0))
                const(pool.affine_select(out=m[:], in_=m[:], compare_op=ALU.not_equal, fill=1.0, base=0,
                                         pattern=[[-1, 128]], channel_multiplier=1))
            const(pool.memset(causal[:], 0.0))
            const(pool.affine_select(out=causal[:], in_=causal[:], compare_op=ALU.is_ge, fill=MASKED, base=0,
                                     pattern=[[0, HJ], [-1, T]], channel_multiplier=1))
            const(pool.memset(ones_r[:].bitcast(fp32), 1.0))
            const(pool.memset(eps[:], EPS))
            const(pool.memset(one_row[:], 1.0))
            for r in range(3):
                part = slot_rows[QF * r:QF * r + QF, :]
                const(pool.memset(part, 1.0))
                const(pool.affine_select(out=part, in_=part, compare_op=ALU.is_ge, fill=0.0, base=0,
                                         pattern=[[-HD, HJ]], channel_multiplier=1))
                const(pool.affine_select(out=part, in_=part, compare_op=ALU.is_ge, fill=0.0, base=HD - 1,
                                         pattern=[[HD, HJ]], channel_multiplier=-1))
            const(pool.memset(vst[:], 0.0))
            const(pool.memset(vst[:, :, :, HD:HD + 1], 1.0))
            assert consts[0] == CONSTS

            def norm_x(g):
                w.ge_group(x_normed, g + 1)
                if g == 0:
                    pool.wait_ge(setup_done, 1)
                part = res[:, bass.ds(w.batch(g * GB), GB), :]
                pool.tensor_tensor(part, part, bias1[:].rearrange("p (a c) -> p a c", a=1).broadcast_to([T, GB, C]), ALU.add)\
                    .then_inc(xbias_added, 1)

            def stacks(b):
                w.ge(stacked, b + 1)
                w.ge(scored_t, NJ * (b - 3), NJ)
                w.alone()
                for i in range(HJ):
                    ins = pool.tensor_scalar(q_slots[:, b % 4, :, i, :], qk_stack[:, b % 4, 0:NJ, :].bitcast(fp32),
                                             slot_rows[:, i:i + 1], None, ALU.mult)
                ins.then_inc(q_slotted, 1)

            def scores(b, j):
                if j < NJ - 1:
                    return
                w.ge(maxed, NJ * (b + 1), NJ)
                w.ge(scored_t, NJ * b, NJ)
                w.alone()
                pool.affine_select(out=dmax[:], in_=negmax[:, b % 2, :].rearrange("p (h a) -> p h a", a=1).broadcast_to([T, NH, T]),
                                   compare_op=ALU.is_equal, fill=0.0, base=0, pattern=[[0, NH], [1, T]],
                                   channel_multiplier=-1).then_inc(diag_ready, 1)

            def scores_t(b, j):
                w.ge(exped, NJ * b + j + 1, NJ)
                w.alone()
                part = probs[:, b % 2, j * HJ:(j + 1) * HJ, :]
                pool.affine_select(out=part, in_=part, compare_op=ALU.is_ge, fill=0.0, base=0,
                                   pattern=[[0, HJ], [1, T]], channel_multiplier=-1).then_inc(probs_ready, 1)

            def attn_out(b):
                w.bank_read(("attn_out", b))
                w.bank_read(("xout", b - 4))
                pool.tensor_tensor(x1b[:, b % 4, :], x1[:, b % 4, :], bias2[:], ALU.add).then_inc(x1b_ready, 1)

            w.run({"norm_x": norm_x, "stacks": stacks, "scores": scores, "scores_t": scores_t,
                   "attn_out": attn_out})

            pool.wait_ge(wgu_in, 16 * 2 * NE)
            pool.wait_ge(scored_t, NJ * B)
            for e in range(NE):
                raw = t_qk[:, e, :] if e < E else xT[:]
                step(pool.tensor_scalar(wgu_hi[:, e, :], raw, 1.0, None, ALU.mult))
                pool.tensor_tensor(wgu_lo[:, e, :], raw, wgu_hi[:, e, :].bitcast(fp32), ALU.subtract).then_inc(wgu_split, 1)

        @block.tensor
        def _(pe):
            w = Waits(pe)
            pe.wait_ge(const_ready, CONSTS)
            pe.wait_ge(w_in, 16 * W_LOADS)
            for k in range(3):
                pe.transpose(PM[0][:, k * C:(k + 1) * C], wa[:, k, :], ident[:])
            pe.transpose(PM[0][:, 3 * C:4 * C], wsq[:, 0, :], ident[:]).then_inc(filled[0], 1)
            pe.transpose(PM[1][:, 0:C], wsq[:, 4, :], ident[:])
            pe.transpose(PM[1][:, C:C + NE], wr[:], ident[0:NE, 0:NE]).then_inc(filled[1], 1)
            pe.matmul(PM[2][:, 0:C], wsq[:, 3, :], wsq[:, 1, :], start=True, stop=True)
            pe.matmul(PM[2][:, C:C + 1], wsq[:, 1, :], cols[:, 2:3], start=True, stop=True).then_inc(filled[2], 1)
            pe.wait_ge(drained[0], 1)
            pe.wait_ge(drained[1], 1)
            pe.matmul(PM[3][:, 0:C], wsq[:, 2, :], woT[:], start=True, stop=True)
            pe.matmul(PM[3][:, C:2 * C], bcol[:, 0, :], wpT[:], start=True, stop=False)
            pe.matmul(PM[3][:, C:2 * C], one_row[:], rows[:, 0, :], start=False, stop=True)
            pe.matmul(PM[3][:, 2 * C:3 * C], bcol[:, 1, :], woT[:], start=True, stop=False)
            pe.matmul(PM[3][:, 2 * C:3 * C], one_row[:], rows[:, 1, :], start=False, stop=True).then_inc(filled[3], 1)

            def turn_x(g):
                bank = w.bank_free(("turn_x", g))
                w.ge_group(x_normed, g + 1)
                for u in range(GB):
                    mm = pe.transpose(bank[:, u * T:(u + 1) * T], xn1[:, u, :], ident[:])
                mm.then_inc(put_bank(("turn_x", g)), 1)

            def project(g, n):
                col = (n + NJ) % (2 * NJ)
                bank = w.bank_free(("project", g, n))
                w.ge_group(xT_split, g + 1)
                if g == 0 and n == 0:
                    pe.wait_ge(setup_done, 1)
                parts = ((wqk_hi, xT_hi), (wqk_hi, xT_lo), (wqk_lo, xT_hi))
                for k, (a, m) in enumerate(parts):
                    mm = pe.matmul(bank[0:KR, :], a[:, col].rearrange("p r f -> p (r f)"), m[:, 0, :], start=(k == 0), stop=(k == 2))
                mm.then_inc(put_bank(("project", g, n)), 1)

            def project_v(b):
                bank = w.bank_free(("project_v", b))
                if b < 2:
                    pe.wait_ge(xT_split, 1)
                    pe.wait_ge(setup_done, 1)
                pe.matmul(bank[:, 0:C], xT[:, (b % GB) * T:(b % GB + 1) * T], wvT[:], start=True, stop=True)\
                    .then_inc(put_bank(("project_v", b)), 1)

            def scores(b, j):
                n = NJ * b + j
                w.ge(maxed, n - 1, NJ)
                if j == 0:
                    w.ge(k_slotted, b + 1)
                pe.matmul(PS[j % 2][:], ident16[:], causal[:].rearrange("p a t -> p (a t)"), start=True, stop=False)
                pe.matmul(PS[j % 2][:], qk_stack[:, b % 4, j, :], k_slots[:, b % 2, j].rearrange("p a t -> p (a t)"), start=False, stop=True)\
                    .then_inc(scored, 1)

            def scores_t(b, j):
                n = NJ * b + j
                w.ge(exped, n - 1, NJ)
                if j == 0:
                    w.ge(diag_ready, b + 1)
                    w.ge(q_slotted, b + 1)
                pe.matmul(PT[j % 2][:], ones_r[:], dmax[:, j * HJ:(j + 1) * HJ, :].rearrange("p a t -> p (a t)"),
                          start=True, stop=False)
                pe.matmul(PT[j % 2][:], qk_stack[:, b % 4, NJ + j, :], q_slots[:, b % 4, j].rearrange("p a t -> p (a t)"),
                          start=False, stop=True).then_inc(scored_t, 1)

            def values(b):
                bank = w.bank_free(("values", b))
                w.ge(probs_ready, NJ * (b + 1), NJ)
                w.bank_read(("project_v", b))
                for j in range(NJ):
                    for i in range(HJ):
                        h = j * HJ + i
                        mm = pe.matmul(bank[VW * i:VW * (i + 1), j * T:(j + 1) * T], vst[:, b % 4, h, :],
                                       probs[:, b % 2, h, :], start=True, stop=True, skip_group_check=True)
                mm.then_inc(put_bank(("values", b)), 1)

            def tall_sums(b):
                bank = w.bank_free(("tall_sums", b))
                w.bank_read(("values", b))
                for j in range(NJ):
                    mm = pe.transpose(bank[:, j * T:(j + 1) * T], yu[:, j * T:(j + 1) * T], ident[:])
                mm.then_inc(put_bank(("tall_sums", b)), 1)

            def turn_y(b):
                bank = w.bank_free(("turn_y", b))
                w.bank_read(("tall_sums", b))
                pe.transpose(bank[:, 0:T], yn[:], ident[:]).then_inc(put_bank(("turn_y", b)), 1)

            def attn_out(b):
                bank = w.bank_free(("attn_out", b))
                w.bank_read(("turn_y", b))
                pe.matmul(bank[:, 0:C], ynT[:], wpT[:], start=True, stop=True).then_inc(put_bank(("attn_out", b)), 1)

            def turn_x2(b):
                bank = w.bank_free(("turn_x2", b))
                w.ge(xn2_ready, b + 1)
                pe.wait_ge(ctx_loaded[b % 4], w.count(16 * (b // 4 + 1), 16))
                pe.transpose(bank[:, 0:T], xn2[:], ident[:])
                pe.transpose(bank[:, T:2 * T], ctx_t[:, b % 4, :], ident[:])\
                    .then_inc(put_bank(("turn_x2", b)), 1)

            def xproject(b):
                bank = w.bank_free(("xproject", b))
                w.bank_read(("turn_x2", b))
                pe.matmul(bank[:, 0:T], wA[:], xcT[:, b % 2, 0, :], start=True, stop=True)
                pe.matmul(bank[:, T:2 * T], xcT[:, b % 2, 1, :], wM[:], start=True, stop=True)\
                    .then_inc(put_bank(("xproject", b)), 1)

            def xscores(b):
                bank = w.bank_free(("xscores", b))
                w.bank_read(("xproject", b))
                pe.matmul(bank[:, 0:T], qa[:], xcT[:, b % 2, 1, :], start=True, stop=True)\
                    .then_inc(put_bank(("xscores", b)), 1)

            def turn_xprobs(b):
                bank = w.bank_free(("turn_xprobs", b))
                w.bank_read(("xscores", b))
                pe.transpose(bank[:, 0:T], xprobs[:], ident[:]).then_inc(put_bank(("turn_xprobs", b)), 1)

            def xout(b):
                bank = w.bank_free(("xout", b))
                w.bank_read(("turn_xprobs", b))
                pe.matmul(bank[:, 0:C], xprobsT[:], cm[:, b % 2, :], start=True, stop=True)\
                    .then_inc(put_bank(("xout", b)), 1)

            def turn_ffn(b):
                bank = w.bank_free(("turn_ffn", b))
                w.ge(xn3_ready, b + 1)
                pe.transpose(bank[:, 0:T], xn3[:], ident[:]).then_inc(put_bank(("turn_ffn", b)), 1)

            def router(b):
                bank = w.bank_free(("router", b))
                w.bank_read(("turn_ffn", b))
                pe.matmul(bank[:, 0:NE], x3s[:], wrT[:], start=True, stop=True).then_inc(put_bank(("router", b)), 1)

            w.run(dict(turn_x=turn_x, project=project, project_v=project_v, scores=scores, scores_t=scores_t,
                       values=values, tall_sums=tall_sums, turn_y=turn_y, attn_out=attn_out, turn_x2=turn_x2,
                       xproject=xproject, xscores=xscores, turn_xprobs=turn_xprobs, xout=xout, turn_ffn=turn_ffn,
                       router=router))

            pe.wait_ge(maxed, NJ * B)
            pe.wait_ge(exped, NJ * B)
            for k in range(2):
                pe.wait_ge(drained[k], FILLS[k])
            pe.wait_ge(wd_in, 16 * NE)
            pe.wait_ge(wgu_split, NE)

            def gate_up(n, base, g2):
                e, k = n % NE, n // NE
                if e == 0:
                    pe.wait_ge(xb_split, g2 * 2 + k + 1)
                for f in range(FT):
                    if not (n == 0 and base is None):
                        pe.wait_ge(h_ready, FT * n + f - FT + 1 if base is None else base * FT + (FT * n + f - FT + 1))
                    for dst, col, done in ((PS[f], f * 128, gate_done), (PT[f], FF + f * 128, up_done)):
                        for r, (a, m) in enumerate(((wgu_hi, xT_hi), (wgu_hi, xT_lo), (wgu_lo, xT_hi))):
                            mm = pe.matmul(dst[:], a[:, e, col:col + 128], m[:, k, :], start=(r == 0), stop=(r == 2))
                        mm.then_inc(done, 1)

            def down(n, base):
                e = n % NE
                pe.wait_ge(h_ready, FT * (n + 1) if base is None else base * FT + FT * (n + 1))
                if not (n < 2 and base is None):
                    pe.wait_ge(mixed, n - 1 if base is None else base + (n - 1))
                for f in range(FT):
                    for t in range(GB):
                        mm = pe.matmul(PM[n % 2][:, t * C:(t + 1) * C], h_all[:, n % 2, f, t * T:(t + 1) * T],
                                       wd[:, e, f, :], start=(f == 0 and t == 0), stop=(f == FT - 1 and t == GB - 1),
                                       skip_group_check=True)
                mm.then_inc(down_done, 1)

            def pair(g2, base):
                for n in range(2 * NE):
                    gate_up(n, base, g2)
                    if n:
                        down(n - 1, base)
                down(2 * NE - 1, base)

            pair(0, None)
            with pe.Fori(1, NG // 2) as g2:
                pair(g2, g2 * (2 * NE))

        @block.scalar
        def _(act):
            w = Waits(act)

            def norm_x_stats(g):
                w.ge_group(x_stats, g + 1)
                if g == 0:
                    act.wait_ge(const_ready, CONSTS)
                act.activation(ln1[:], mv1[:, :, 1], ACT.Ln, bias=eps[:, 0:1]).then_inc(x_ln, 1)
                w.ge_group(x_ln, g + 1)
                act.activation(rs1[:], ln1[:], ACT.Exp, scale=-0.5).then_inc(x_rstd, 1)

            def turn_x(g):
                bank, drain = w.bank_filled(("turn_x", g))
                act.activation(xT[:], bank[:], ACT.Copy).then_inc(drain, 1)

            def stacks(b):
                u = b % GB
                w.bank_read(("project", b // GB, 7))
                w.ge(scored_t, NJ * (b - 3), NJ)
                act.activation(qk_stack[:, b % 4], t_qk[0:KR, :, u * T:(u + 1) * T], ACT.Copy).then_inc(rounded, 1)

            def project_v(b):
                bank, drain = w.bank_filled(("project_v", b))
                act.activation(vst[:, b % 4, :, 0:HD], bank[:, 0:C].rearrange("p (h d) -> p h d", d=HD), ACT.Copy)\
                    .then_inc(drain, 1)

            def scores_t(b, j):
                w.ge(scored_t, NJ * b + j + 1, NJ)
                act.activation(probs[:, b % 2, j * HJ:(j + 1) * HJ, :].rearrange("p a t -> p (a t)"), PT[j % 2][:], ACT.Exp)\
                    .then_inc(exped, 1)

            def values(b):
                bank, drain = w.bank_filled(("values", b))
                w.bank_read(("tall_sums", b - 1))
                act.activation(yu[:], bank[:], ACT.Copy).then_inc(drain, 1)

            def turn_y(b):
                bank, drain = w.bank_filled(("turn_y", b))
                w.bank_read(("attn_out", b - 1))
                act.activation(ynT[:], bank[:, 0:T], ACT.Copy).then_inc(drain, 1)

            def attn_out(b):
                w.ge(x1_stats, b + 1)
                act.activation(ln2[:], mv2[:, 1:2], ACT.Ln, bias=eps[:, 0:1]).then_inc(x1_ln, 1)
                w.ge(x1_ln, b + 1)
                act.activation(rs2[:], ln2[:], ACT.Exp, scale=-0.5).then_inc(x1_rstd, 1)

            def turn_x2(b):
                bank, drain = w.bank_filled(("turn_x2", b))
                act.activation(xcT[:, b % 2].rearrange("p a t -> p (a t)"), bank[:, 0:2 * T], ACT.Copy).then_inc(drain, 1)

            def xproject(b):
                bank, drain = w.bank_filled(("xproject", b))
                w.bank_read(("xout", b - 2))
                act.activation(qa[:], bank[:, 0:T], ACT.Identity, bias=bqA[:, 0:1])
                act.activation(cm[:, b % 2, :], bank[:, T:2 * T], ACT.Copy).then_inc(drain, 1)

            def xscores(b):
                bank, drain = w.bank_filled(("xscores", b))
                w.ge(xneg_ready, b + 1)
                w.bank_read(("turn_xprobs", b - 1))
                act.activation(xprobs[:], bank[:, 0:T], ACT.Exp, bias=xneg[:, 0:1], accum_out=xsum[:, b % 2, :]).then_inc(drain, 1)

            def xout(b):
                w.ge(x2_stats, b + 1)
                act.activation(ln3[:], mv3[:, 1:2], ACT.Ln, bias=eps[:, 0:1]).then_inc(x2_ln, 1)
                w.ge(x2_ln, b + 1)
                act.activation(rs3[:], ln3[:], ACT.Exp, scale=-0.5).then_inc(x2_rstd, 1)

            def turn_ffn(b):
                bank, drain = w.bank_filled(("turn_ffn", b))
                w.bank_read(("router", b - 1))
                act.activation(x3s[:], bank[:, 0:T], ACT.Copy).then_inc(drain, 1)

            w.run(dict(norm_x_stats=norm_x_stats, turn_x=turn_x, stacks=stacks, project_v=project_v,
                       scores_t=scores_t, values=values, turn_y=turn_y, attn_out=attn_out, turn_x2=turn_x2,
                       xproject=xproject, xscores=xscores, xout=xout, turn_ffn=turn_ffn))

            act.wait_ge(centred, 1)
            act.activation(cw[:], cw[:], ACT.Exp).then_inc(route_exped, 1)

            def group(base):
                for n in range(2 * NE):
                    for f in range(FT):
                        m = FT * n + f
                        act.wait_ge(gate_done, m + 1 if base is None else base * FT + (m + 1))
                        if not (n == 0 and base is None):
                            act.wait_ge(h_ready, m - FT + 1 if base is None else base * FT + (m - FT + 1))
                        act.activation(silu[:, f, :], PS[f][:], ACT.Silu).then_inc(silu_done, 1)

            group(None)
            with act.Fori(1, NG // 2) as g2:
                group(g2 * (2 * NE))

        @block.vector
        def _(dve):
            w = Waits(dve)
            steps = [0]

            def step(ins):
                steps[0] += 1
                ins.then_inc(dve_step, 1)
                dve.wait_ge(dve_step, steps[0])

            dve.wait_ge(w_in, 16 * W_LOADS)
            step(dve.tensor_copy(bcol, cols[:, 0:2].rearrange("p (k a) -> p k a", a=1).broadcast_to([C, 2, C])))
            dve.wait_ge(filled[1], 1)
            dve.tensor_copy(woT[:], PM[1][:, 0:C])
            dve.tensor_copy(wrT[:], PM[1][:, C:C + NE]).then_inc(drained[1], 1)
            dve.wait_ge(filled[0], 1)
            dve.tensor_copy(wqkT.rearrange("p k c -> p (k c)"), PM[0][:, 0:2 * C])
            dve.tensor_copy(wvT[:], PM[0][:, 2 * C:3 * C])
            dve.tensor_copy(wpT[:], PM[0][:, 3 * C:4 * C]).then_inc(drained[0], 1)
            dve.wait_ge(drained[0], 1)
            wqk = wqkT.rearrange("p k (j a f) -> p (k j) a f", j=NJ, a=1).broadcast_to([C, 2 * NJ, 3, QF])
            step(dve.tensor_copy(wqk_hi[:], wqk))
            dve.tensor_tensor(wqk_lo[:], wqk, wqk_hi[:].bitcast(fp32), ALU.subtract)
            dve.wait_ge(filled[2], 1)
            dve.tensor_scalar(wA[:], PM[2][:, 0:C], XSCALE, None, ALU.mult)
            dve.tensor_scalar(bqA[:], PM[2][:, C:C + 1], XSCALE, None, ALU.mult).then_inc(drained[2], 1)
            dve.wait_ge(filled[3], 1)
            dve.tensor_copy(wM[:], PM[3][:, 0:C])
            dve.tensor_copy(bias1[:], PM[3][:, C:2 * C])
            dve.tensor_copy(bias2[:], PM[3][:, 2 * C:3 * C]).then_inc(drained[3], 1)
            dve.wait_ge(drained[3], 1)
            dve.memset(gexp[:], 0.0).then_inc(setup_done, 1)

            def norm_x_stats(g):
                if g == 0:
                    dve.wait_ge(x_in[0], 16)
                elif g == 1:
                    dve.wait_ge(x_in[1], 16)
                for u in range(GB):
                    ins = dve.bn_stats(st1[:, u, :], res[:, bass.ds(w.batch(g * GB + u), 1), :].rearrange("p a c -> p (a c)"))
                ins.then_inc(x_part, 1)
                w.ge_group(x_part, g + 1)
                w.alone()
                for u in range(GB):
                    ins = dve.bn_aggr(mv1[:, u, :], st1[:, u, :])
                ins.then_inc(x_stats, 1)

            def norm_x(g):
                w.ge_group(x_rstd, g + 1)
                for u in range(GB):
                    ins = dve.tensor_scalar(xn1[:, u, :], res[:, bass.ds(w.batch(g * GB + u), 1), :].rearrange("p a c -> p (a c)"),
                                            mv1[:, u, 0:1], rs1[:, u:u + 1], ALU.subtract, ALU.mult)
                ins.then_inc(x_normed, 1)

            def turn_x(g):
                w.bank_read(("turn_x", g))
                dve.tensor_copy(xT_hi[:, 0, :], xT[:]).then_inc(xhi_done, 1)
                w.ge_group(xhi_done, g + 1)
                dve.tensor_tensor(xT_lo[:, 0, :], xT[:], xT_hi[:, 0, :].bitcast(fp32), ALU.subtract).then_inc(xT_split, 1)

            def project(g, n):
                bank, drain = w.bank_filled(("project", g, n))
                col = (n + NJ) % (2 * NJ)
                w.ge(rounded, g * GB)
                dve.scalar_tensor_tensor(out=t_qk[0:KR, col, :].rearrange("p (u t) -> p u t", u=GB),
                                         in0=bank[0:KR, :].rearrange("p (u t) -> p u t", u=GB), scalar=bqk[:, col:col + 1],
                                         in1=ropes[:, col // NJ, :].rearrange("p (a t) -> p a t", a=1).broadcast_to([KR, GB, T]),
                                         op0=ALU.add, op1=ALU.mult).then_inc(drain, 1)

            def stacks(b):
                u = b % GB
                w.ge(rounded, b + 1)
                for q, cs in ((2, slice(0, NJ)), (1, slice(NJ, 2 * NJ))):
                    part = qk_stack[QF * q:QF * (q + 1), b % 4, cs, :]
                    ins = dve.tensor_tensor(part, t_qk[QF * q:QF * (q + 1), cs, u * T:(u + 1) * T], part.bitcast(fp32),
                                            ALU.subtract)
                ins.then_inc(stacked, 1)
                w.ge(stacked, b + 1)
                w.ge(scored, NJ * (b - 1), NJ)
                for i in range(HJ):
                    ins = dve.tensor_scalar(k_slots[:, b % 2, :, i, :], qk_stack[:, b % 4, NJ:, :].bitcast(fp32),
                                            slot_rows[:, i:i + 1], None, ALU.mult)
                ins.then_inc(k_slotted, 1)

            def scores(b, j):
                w.ge(scored, NJ * b + j + 1, NJ)
                if j == 0:
                    w.ge(diag_ready, b - 1)
                dve.reduce_max(negmax[:, b % 2, j * HJ:(j + 1) * HJ], PS[j % 2][:].rearrange("p (i t) -> p i t", i=HJ),
                               axis=AX.X, negate=True).then_inc(maxed, 1)

            def tall_sums(b):
                bank, drain = w.bank_filled(("tall_sums", b))
                heads = bank[:].rearrange("p (h v) -> p h v", v=VW)
                dve.reciprocal(ysum[:].rearrange("p (h a) -> p h a", a=1), heads[:, :, HD:HD + 1]).then_inc(y_inverse, 1)
                w.ge(y_inverse, b + 1)
                w.bank_read(("turn_y", b - 1))
                dve.tensor_tensor(yn[:].rearrange("p (h d) -> p h d", d=HD), heads[:, :, 0:HD],
                                  ysum[:].rearrange("p (h a) -> p h a", a=1).broadcast_to([T, NH, HD]), ALU.mult)\
                    .then_inc(drain, 1)

            def one(b):
                return res[:, bass.ds(w.batch(b), 1), :].rearrange("p a c -> p (a c)")

            def attn_out(b):
                bank, drain = w.bank_filled(("attn_out", b))
                w.ge_group(xbias_added, b // GB + 1)
                w.ge(x1b_ready, b - 3)
                dve.tensor_tensor(x1[:, b % 4, :], bank[:, 0:C], one(b), ALU.add).then_inc(drain, 1)
                w.bank_read(("attn_out", b))
                w.alone()
                dve.bn_stats(st2[:], x1[:, b % 4, :]).then_inc(x1_part, 1)
                w.ge(x1_part, b + 1)
                w.alone()
                dve.bn_aggr(mv2[:], st2[:]).then_inc(x1_stats, 1)

            def norm_xattn(b):
                w.ge(x1_rstd, b + 1)
                w.bank_read(("turn_x2", b - 1))
                dve.tensor_scalar(xn2[:], x1[:, b % 4, :], mv2[:, 0:1], rs2[:, 0:1], ALU.subtract, ALU.mult)\
                    .then_inc(xn2_ready, 1)

            def xscores(b):
                bank, _ = w.bank_filled(("xscores", b))
                w.bank_read(("xscores", b - 1))
                dve.reduce_max(xneg[:], bank[:, 0:T], axis=AX.X, negate=True).then_inc(xneg_ready, 1)

            def turn_xprobs(b):
                bank, drain = w.bank_filled(("turn_xprobs", b))
                dve.reciprocal(xinv[:], xsum[:, b % 2, :]).then_inc(x_inverse, 1)
                dve.tensor_copy(xprobsT[:], bank[:, 0:T]).then_inc(drain, 1)

            def xout(b):
                bank, drain = w.bank_filled(("xout", b))
                w.ge(x_inverse, b + 1)
                w.ge(x1b_ready, b + 1)
                dve.scalar_tensor_tensor(out=one(b), in0=bank[:, 0:C], scalar=xinv[:, 0:1], in1=x1b[:, b % 4, :],
                                         op0=ALU.mult, op1=ALU.add).then_inc(drain, 1)
                w.bank_read(("xout", b))
                w.alone()
                dve.bn_stats(st3[:], one(b)).then_inc(x2_part, 1)
                w.ge(x2_part, b + 1)
                w.alone()
                dve.bn_aggr(mv3[:], st3[:]).then_inc(x2_stats, 1)

            def norm_ffn(b):
                w.ge(x2_rstd, b + 1)
                w.bank_read(("turn_ffn", b - 1))
                dve.tensor_scalar(xn3[:], one(b), mv3[:, 0:1], rs3[:, 0:1], ALU.subtract, ALU.mult).then_inc(xn3_ready, 1)

            def turn_ffn(b):
                w.bank_read(("turn_ffn", b))
                dve.tensor_copy(x3T[:, bass.ds(w.batch(b) * T, T)], x3s[:]).then_inc(x3T_kept, 1)

            def router(b):
                bank, drain = w.bank_filled(("router", b))
                dve.tensor_copy(logit[:, bass.ds(w.batch(b), 1), :].rearrange("p a e -> p (a e)"), bank[:, 0:NE])\
                    .then_inc(drain, 1)

            w.run(dict(norm_x_stats=norm_x_stats, norm_x=norm_x, turn_x=turn_x, project=project, stacks=stacks,
                       scores=scores, tall_sums=tall_sums, attn_out=attn_out, norm_xattn=norm_xattn, xscores=xscores,
                       turn_xprobs=turn_xprobs, xout=xout, norm_ffn=norm_ffn, turn_ffn=turn_ffn, router=router))

            lg, ex = logit[:, :, 0:E], cw[:, :, 0:E]
            last = FILL[("router", B - 1)]
            dve.wait_ge(drained[last[0]], last[1] + 1)
            for e in range(E):
                ins = dve.memset(ramp[:, :, e:e + 1], float(E - e))
            step(ins)
            step(dve.reduce_max(top_p[:].rearrange("p b a -> p (b a)"), lg, axis=AX.X))
            step(dve.tensor_tensor(ex, lg, top_p[:].broadcast_to([T, B, E]), ALU.subtract))
            dve.tensor_scalar(cw[:, :, E:NE], logit[:, :, E:NE], -1.0, None, ALU.mult).then_inc(centred, 1)
            dve.wait_ge(route_exped, 1)
            step(dve.reduce_sum(top_p[:].rearrange("p b a -> p (b a)"), ex, axis=AX.X))
            step(dve.reciprocal(gexp[:], top_p[:]))
            step(dve.tensor_tensor(pick, ex, gexp[:].broadcast_to([T, B, E]), ALU.mult))
            left = pick
            for k, sel in enumerate((sel1, sel2)):
                step(dve.reduce_max(top_p[:].rearrange("p b a -> p (b a)"), left, axis=AX.X))
                step(dve.tensor_tensor(sel, left, top_p[:].broadcast_to([T, B, E]), ALU.is_ge))
                step(dve.tensor_tensor(sel, sel, ramp, ALU.mult))
                step(dve.reduce_max(top_p[:].rearrange("p b a -> p (b a)"), sel, axis=AX.X))
                step(dve.tensor_tensor(sel, ramp, top_p[:].broadcast_to([T, B, E]), ALU.is_equal))
                if k == 0:
                    step(dve.scalar_tensor_tensor(out=rest, in0=sel1, scalar=-2.0, in1=pick, op0=ALU.mult, op1=ALU.add))
                    left = rest
            step(dve.tensor_tensor(sel1, sel1, sel2, ALU.add))
            step(dve.tensor_tensor(ex, sel1, pick, ALU.mult))
            step(dve.tensor_scalar(gexp[:], cw[:, :, E:NE], 1.0, None, ALU.add))
            step(dve.reciprocal(cw[:, :, E:NE], gexp[:]))

            def group(g2, base):
                for n in range(2 * NE):
                    e, k = n % NE, n // NE
                    g = g2 * 2 + k
                    if e == 0:
                        if base is not None:
                            dve.wait_ge(up_done, (base + (n - NE)) * FT)
                        src = x3T[:, bass.ds(g * (GB * T), GB * T)]
                        dve.tensor_copy(xT_hi[:, k, :], src).then_inc(xb_hi_done, 1)
                        dve.wait_ge(xb_hi_done, g + 1)
                        dve.tensor_tensor(xT_lo[:, k, :], src, xT_hi[:, k, :].bitcast(fp32), ALU.subtract).then_inc(xb_split, 1)
                    for f in range(FT):
                        m = FT * n + f + 1
                        dve.wait_ge(silu_done, m if base is None else base * FT + m)
                        dve.wait_ge(up_done, m if base is None else base * FT + m)
                        if not (n < 2 and base is None):
                            dve.wait_ge(down_done, n - 1 if base is None else base + (n - 1))
                        dve.tensor_tensor(h_all[:, n % 2, f, :], silu[:, f, :], PT[f][:], ALU.mult).then_inc(h_ready, 1)
                    if n:
                        mix(g2, base, n - 1)
                mix(g2, base, 2 * NE - 1)

            def mix(g2, base, n):
                e, g = n % NE, g2 * 2 + n // NE
                dve.wait_ge(down_done, n + 1 if base is None else base + (n + 1))
                if not (n == 0 and base is None):
                    dve.wait_ge(mixed, n if base is None else base + n)
                for t in range(GB):
                    part = res[:, bass.ds(g * GB + t, 1), :].rearrange("p a c -> p (a c)")
                    ins = dve.scalar_tensor_tensor(out=part, in0=PM[n % 2][:, t * C:(t + 1) * C],
                                                   scalar=cw[:, bass.ds(g * GB + t, 1), e:e + 1].rearrange("p a e -> p (a e)"),
                                                   in1=part, op0=ALU.mult, op1=ALU.add)
                ins.then_inc(mixed, 1)

            group(0, None)
            with dve.Fori(1, NG // 2) as g2:
                group(g2, g2 * (2 * NE))


NAMES = ['x', 'ctx_1024', 'L0_attn_W_attn', 'L0_attn_b_attn', 'L0_attn_W_proj', 'L0_attn_b_proj', 'L0_xattn_Wk',
         'L0_xattn_Wv', 'L0_xattn_bv', 'L0_xattn_Wq', 'L0_xattn_bq', 'L0_xattn_Wo', 'L0_xattn_bo', 'L0_ffn_router_w',
         'L0_ffn_w_gate', 'L0_ffn_w_up', 'L0_ffn_w_down', 'L0_ffn_sw_gate', 'L0_ffn_sw_up', 'L0_ffn_sw_down',
         'L0_ffn_gate_w']


def rotary_factors():
    import numpy as np
    theta = (1.0 / np.float32(10000.0) ** (np.float32(2.0) * np.arange(HD // 2, dtype=np.float32) / HD)).astype(np.float32)
    ang = (np.arange(1, T + 1, dtype=np.float32)[None, :] * theta[:, None]).astype(np.float32)
    f = (np.cos(ang) + np.sin(ang)).astype(np.float32)
    f = f[np.arange(KR) % (HD // 2)]
    return np.stack([f * np.float32(QSCALE), f], axis=1).astype(np.float32)


def kernel(**inputs):
    import numpy as np
    import concourse.bacc as bacc
    from concourse.bass_utils import run_bass_kernel_spmd

    nc = bacc.Bacc("TRN2", target_bir_lowering=False, num_devices=1)
    arrays, args = {}, []
    for name, a in [(n, np.ascontiguousarray(inputs[n])) for n in NAMES] + [("rotary", rotary_factors())]:
        arrays[f"in_{name}"] = a
        args.append(nc.dram_tensor(f"in_{name}", a.shape, mybir.dt.from_np(a.dtype), kind="ExternalInput").ap())
    args.append(nc.dram_tensor("out_x", (B, T, C), fp32, kind="ExternalOutput").ap())
    build(nc, *args)
    return run_bass_kernel_spmd(nc, [arrays], core_ids=[0]).results[0]["out_x"]
```

```python
from contextlib import ExitStack

import concourse.bass as bass
from concourse import mybir

fp32 = mybir.dt.float32
fp32r = mybir.dt.float32r
bf16 = mybir.dt.bfloat16
ALU = mybir.AluOpType
ACT = mybir.ActivationFunctionType
AX = mybir.AxisListType

B = 32
T = 128
C = 128
NH = 16
HD = C // NH
GB = 4
NG = B // GB
HJ = 4
NJ = NH // HJ
HR = 3 * HD
KR = HJ * HR
VW = 32
E = 8
FF = 256
NE = E + 1
FT = FF // 128
EPS = 1e-5
QSCALE = HD ** -0.5
XSCALE = C ** -0.5
MASKED = -3.0e38

ORDER = [
    ("turn_x", 2, None, 0),
    ("turn_ffn", -7, None, None),
    ("stacks", 1, None, 0),
    ("rstd_x", 3, None, 0),
    ("scores_t", -2, 2, None),
    ("turn_max", -1, None, None),
    ("scores_t", -2, 3, None),
    ("xscores", -5, None, None),
    ("router", -7, None, None),
    ("stack_lo", 1, None, 3),
    ("stack_lo", 1, None, 1),
    ("stack_lo", 1, None, 2),
    ("stack_lo", 1, None, 0),
    ("scores", 0, 0, None),
    ("project_v", 1, None, 2),
    ("turn_y", -3, None, None),
    ("project", 2, 5, 0),
    ("turn_x2", -4, None, None),
    ("stacks", 2, None, 3),
    ("norm_x", 3, None, 0),
    ("stacks", 2, None, 2),
    ("project_v", 1, None, 0),
    ("scores", 0, 1, None),
    ("project_v", 1, None, 1),
    ("stacks", 2, None, 1),
    ("rstd_ffn", -6, None, None),
    ("attn_out", -3, None, None),
    ("turn_xprobs", -5, None, None),
    ("values", -2, None, None),
    ("project", 2, 1, 0),
    ("project", 2, 3, 0),
    ("project_v", 2, None, 3),
    ("project", 2, 6, 0),
    ("rstd_xattn", -3, None, None),
    ("norm_ffn", -6, None, None),
    ("norm_x_stats", 4, None, 0),
    ("norm_xattn", -3, None, None),
    ("scores", 0, 2, None),
    ("scores", 0, 3, None),
    ("project", 2, 0, 0),
    ("xproject", -4, None, None),
    ("scores_t", -1, 0, None),
    ("project", 2, 4, 0),
    ("project", 2, 2, 0),
    ("project", 2, 7, 0),
    ("xout", -5, None, None),
    ("scores_t", -1, 1, None),
    ("tall_sums", -2, None, None),
]
GROUP_STAGES = ("norm_x_stats", "rstd_x", "norm_x", "turn_x", "project")
FIRST_SLOT = -max(ahead for _, ahead, _, _ in ORDER)
END_SLOT = B - min(ahead for _, ahead, _, _ in ORDER)
STEADY = (12, 28)


def timeline(s):
    out = []
    for name, ahead, part, which in ORDER:
        b = s + ahead
        if 0 <= b < B and (which is None or b % GB == which):
            out.append((name, b // GB if name in GROUP_STAGES else b) + (() if part is None else (part,)))
    return out


SHARED = 4
CONSTS = 8
STORES = 3
W_LOADS = 16
BANK = {"turn_xprobs": 1, "turn_x": 2, "turn_y": 1, "xproject": 2, "attn_out": 2, "values": 0,
        "xscores": 2, "turn_ffn": 1, "xout": 3, "turn_max": 3, "project_v": 3, "tall_sums": 0,
        "router": 1, "turn_x2": 0, "project": (0, 1, 1, 3, 3, 3, 2, 2)}
SETUP_FILLS = (1, 1, 1, 1)


def bank_fills():
    count, fill = list(SETUP_FILLS), {}
    for item in [x for s in range(FIRST_SLOT, END_SLOT) for x in timeline(s)]:
        name = item[0]
        if name not in BANK:
            continue
        bank = BANK[name][item[2]] if name == "project" else BANK[name]
        fill[item] = (bank, count[bank])
        count[bank] += 1
    return fill, count


FILL, FILLS = bank_fills()
PER_GROUP = [sum(1 for s in range(STEADY[0], STEADY[0] + GB) for x in timeline(s) if x in FILL and FILL[x][0] == k)
             for k in range(SHARED)]


def build(nc, x, ctx_in, W_attn, b_attn, W_proj, b_proj, Wk, Wv, bv, Wq, bq, Wo, bo, router_w,
          w_gate, w_up, w_down, sw_gate, sw_up, sw_down, gate_w, rope, lo_sign, out):
    ctx = ExitStack()
    with ctx:
        def sb(name, shape, dt=fp32):
            return ctx.enter_context(nc.sbuf_tensor(name, shape, dt))

        def sem(name):
            return ctx.enter_context(nc.semaphore(name))

        res = sb("res", [T, B, C])
        x3T = sb("x3T", [C, B * T])
        t_qk = sb("t_qk", [128, 2 * NJ, GB * T])
        qk_stack = sb("qk_stack", [KR + 1, 4, 2 * NJ, T], fp32r)
        wide = sb("wide", [128, 2 * NE * 2 * FF], fp32r)
        q_slots = wide[0:KR + 1, 0:4 * NJ * HJ * T].rearrange("p (r j i t) -> p r j i t", r=4, j=NJ, i=HJ)
        wgu_hi = wide[:, 0:NE * 2 * FF].rearrange("p (e f) -> p e f", e=NE)
        wgu_lo = wide[:, NE * 2 * FF:].rearrange("p (e f) -> p e f", e=NE)
        k_slots = sb("k_slots", [KR, 2, NJ, HJ, T], fp32r)
        negmax = sb("negmax", [T, 2, NH])
        max_rows = sb("max_rows", [NH, T], fp32r)
        probs = sb("probs", [T, 2, NH, T])
        vst = sb("vst", [T, GB, NH, VW])
        xn1 = sb("xn1", [T, GB, C])
        xT = sb("xT", [C, GB * T])
        xT_hi = sb("xT_hi", [C, 2, GB * T], fp32r)
        xT_lo = sb("xT_lo", [C, 2, GB * T], fp32r)
        yu = sb("yu", [T, NJ * T])
        ysum = sb("ysum", [T, NH])
        yn = sb("yn", [T, C])
        ynT = sb("ynT", [C, T])
        x1 = sb("x1", [T, 4, C])
        x1b = sb("x1b", [T, 4, C])
        xn2 = sb("xn2", [T, C])
        ctx_t = sb("ctx_t", [T, 4, C])
        xcT = sb("xcT", [C, 2, 2, T])
        qa = sb("qa", [C, T])
        cm = sb("cm", [T, 2, C])
        xneg = sb("xneg", [T, 1])
        xsum = sb("xsum", [T, 2, 1])
        xinv = sb("xinv", [T, 1])
        xprobs = sb("xprobs", [T, T])
        xprobsT = sb("xprobsT", [T, T])
        xn3 = sb("xn3", [T, C])
        x3s = sb("x3s", [C, T])
        st1 = sb("st1", [T, GB, 6]); mv1 = sb("mv1", [T, GB, 2]); ln1 = sb("ln1", [T, GB]); rs1 = sb("rs1", [T, GB])
        st2 = sb("st2", [T, 6]); mv2 = sb("mv2", [T, 2]); ln2 = sb("ln2", [T, 1]); rs2 = sb("rs2", [T, 1])
        st3 = sb("st3", [T, 6]); mv3 = sb("mv3", [T, 2]); ln3 = sb("ln3", [T, 1]); rs3 = sb("rs3", [T, 1])
        logit = sb("logit", [T, B, NE])

        ident = sb("ident", [128, 128])
        ident16 = sb("ident16", [128, 128], bf16)
        causal = sb("causal", [T, HJ, T], bf16)
        lo_rows = sb("lo_rows", [KR, 2])
        eps = sb("eps", [T, 1])
        ropes = sb("ropes", [KR, 2, T])
        bqk = sb("bqk", [KR, 2 * NJ])
        wr = sb("wr", [NE, C])
        cols = sb("cols", [C, 3])
        rows = sb("rows", [1, 4, C])
        one_row = sb("one_row", [1, 128])
        wqk_hi = sb("wqk_hi", [C, 2 * NJ, KR], fp32r)
        wqk_lo = sb("wqk_lo", [C, 2 * NJ, KR], fp32r)
        wvT = sb("wvT", [C, C]); wpT = sb("wpT", [C, C]); woT = sb("woT", [C, C])
        wrT = sb("wrT", [C, NE])
        wA = sb("wA", [C, C])
        wM = sb("wM", [C, C])
        bqA = sb("bqA", [C, 1])
        bias1 = sb("bias1", [T, C])
        bias2 = sb("bias2", [T, C])
        wd = sb("wd", [128, NE, FT, C])
        flat = probs[:].rearrange("p r h t -> p (r h t)")
        raw = flat[:, 0:12 * C].rearrange("p (k c) -> p k c", c=C)
        wa = raw[:, 0:3, :]
        wsq = raw[:, 3:8, :]
        bcol = raw[:, 8:10, :]
        wqkT = raw[:, 10:12, :]
        brow = flat[0:1, 12 * C:12 * C + 2 * NJ * KR].rearrange("p (k r) -> p k r", r=KR)
        h_all = flat[:, 0:2 * FT * 512].rearrange("p (r f t) -> p r f t", r=2, f=FT)
        silu = flat[:, 2 * FT * 512:3 * FT * 512].rearrange("p (f t) -> p f t", f=FT)
        cw = sb("cw", [T, B, NE])
        top_p = sb("top_p", [T, B, 1]); gexp = sb("gexp", [T, B, 1])
        vflat = vst[:].rearrange("p u h v -> p (u h v)")
        ramp, sel1, sel2, pick, rest = (vflat[:, k * B * E:(k + 1) * B * E].rearrange("p (b e) -> p b e", b=B) for k in range(5))

        PS = [ctx.enter_context(nc.psum_tensor(f"ps_scores{i}", [T, 512], fp32)) for i in range(2)]
        PT = [ctx.enter_context(nc.psum_tensor(f"ps_scores_t{i}", [T, 512], fp32)) for i in range(2)]
        PM = [ctx.enter_context(nc.psum_tensor(f"ps_shared{i}", [T, 512], fp32)) for i in range(SHARED)]

        x_in = [sem("x_in0"), sem("x_in1")]
        w_in = sem("w_in"); wd_in = sem("wd_in"); wgu_in = sem("wgu_in")
        ctx_loaded = [sem(f"ctx_loaded{i}") for i in range(4)]
        out_written = sem("out_written")
        filled = [sem(f"bank_filled{i}") for i in range(SHARED)]
        drained = [sem(f"bank_drained{i}") for i in range(SHARED)]
        const_ready = sem("const_ready"); pool_step = sem("pool_step"); setup_done = sem("setup_done")
        dve_step = sem("dve_step"); q_cleared = sem("q_cleared"); act_step = sem("act_step")
        x_stats = sem("x_stats"); x_rstd = sem("x_rstd"); x_centred = sem("x_centred"); x_normed = sem("x_normed")
        x_part = sem("x_part"); x_ln = sem("x_ln"); xhi_done = sem("xhi_done"); xT_split = sem("xT_split")
        xbias_added = sem("xbias_added")
        rounded = sem("rounded"); stacked = sem("stacked"); 
        q_slotted = [sem(f"q_slotted{i}") for i in range(4)]; k_slotted = [sem(f"k_slotted{i}") for i in range(4)]
        scored = sem("scored"); maxed = sem("maxed"); scored_t = sem("scored_t")
        max_placed = sem("max_placed"); exped = sem("exped"); probs_ready = sem("probs_ready")
        y_inverse = sem("y_inverse")
        x1_part = sem("x1_part"); x1_stats = sem("x1_stats"); x1_ln = sem("x1_ln"); x1_rstd = sem("x1_rstd")
        x1b_ready = sem("x1b_ready"); xn2_ready = sem("xn2_ready"); xneg_ready = sem("xneg_ready")
        x_inverse = sem("x_inverse")
        x2_part = sem("x2_part"); x2_stats = sem("x2_stats"); x2_ln = sem("x2_ln"); x2_rstd = sem("x2_rstd"); x2_centred = sem("x2_centred")
        xn3_ready = sem("xn3_ready");
        centred = sem("centred"); route_exped = sem("route_exped"); cw_ready = sem("cw_ready")
        wgu_split = sem("wgu_split")
        xb_split = sem("xb_split"); xb_hi_done = sem("xb_hi_done")
        gate_done = sem("gate_done"); up_done = sem("up_done"); silu_done = sem("silu_done"); h_ready = sem("h_ready")
        down_done = sem("down_done"); mixed = sem("mixed")

        block = ctx.enter_context(nc.Block())

        class Waits:

            def __init__(self, engine):
                self.engine, self.it = engine, None

            def count(self, n, per_group):
                return n if self.it is None else n + self.it * per_group

            def ge(self, s, n, rate=1):
                if n > 0:
                    self.engine.wait_ge(s, self.count(n, rate * GB))

            def ge_group(self, s, n, rate=1):
                if n > 0:
                    self.engine.wait_ge(s, self.count(n, rate))

            def alone(self):
                if self.it is not None:
                    self.engine.nop(nofuse=True)

            def batch(self, b):
                return b if self.it is None else b + self.it * GB

            def bank_free(self, item):
                bank, n = FILL[item]
                if n:
                    self.engine.wait_ge(drained[bank], self.count(n, PER_GROUP[bank]))
                return PM[bank]

            def bank_filled(self, item):
                bank, n = FILL[item]
                self.engine.wait_ge(filled[bank], self.count(n + 1, PER_GROUP[bank]))
                return PM[bank], drained[bank]

            def bank_read(self, item):
                name, b, *more = item
                if b < 0:
                    return
                bank, n = FILL[item]
                if self.it is not None:
                    step = 1 if name in GROUP_STAGES else GB
                    assert FILL[(name, b + step, *more)][1] - n == PER_GROUP[bank], item
                self.engine.wait_ge(drained[bank], self.count(n + 1, PER_GROUP[bank]))

            def run(self, stages):
                def take(items):
                    for name, *args in items:
                        if name in stages:
                            stages[name](*args)

                for s in range(FIRST_SLOT, STEADY[0]):
                    take(timeline(s))
                with self.engine.Fori(0, (STEADY[1] - STEADY[0]) // GB) as it:
                    self.it = it
                    for s in range(STEADY[0], STEADY[0] + GB):
                        take(timeline(s))
                self.it = None
                for s in range(STEADY[1], END_SLOT):
                    take(timeline(s))

        def put_bank(item):
            return filled[FILL[item][0]]

        @block.sync
        def _(sp):
            w = Waits(sp)
            sp.dma_start(res[:, 0:GB, :], x[0:GB].rearrange("b t c -> t b c")).then_inc(x_in[0], 16)
            sp.dma_start(wa, W_attn.rearrange("(k p) c -> p k c", p=128)).then_inc(w_in, 16)
            for n, m in enumerate((W_proj, Wk, Wv, Wq, Wo)):
                sp.dma_start(wsq[:, n, :], m).then_inc(w_in, 16)
            sp.dma_start(wr[0:E, :], router_w).then_inc(w_in, 16)
            sp.dma_start(wr[E:NE, :], gate_w).then_inc(w_in, 16)
            sp.dma_start(cols[:, 0:1], b_attn[2 * C:3 * C].rearrange("(p a) -> p a", a=1)).then_inc(w_in, 16)
            sp.dma_start(cols[:, 1:2], bv.rearrange("(p a) -> p a", a=1)).then_inc(w_in, 16)
            sp.dma_start(cols[:, 2:3], bq.rearrange("(p a) -> p a", a=1)).then_inc(w_in, 16)
            sp.dma_start(rows[:, 0, :], b_proj.rearrange("(a n) -> a n", a=1)).then_inc(w_in, 16)
            sp.dma_start(rows[:, 1, :], bo.rearrange("(a n) -> a n", a=1)).then_inc(w_in, 16)
            sp.dma_start(rows[:, 2:4, :], b_attn[0:2 * C].rearrange("(a k n) -> a k n", a=1, k=2)).then_inc(w_in, 16)
            sp.dma_start(ropes[:], rope).then_inc(w_in, 16)
            sp.dma_start(lo_rows[:], lo_sign).then_inc(w_in, 16)
            sp.dma_start(res[:, GB:B, :], x[GB:B].rearrange("b t c -> t b c")).then_inc(x_in[1], 16)
            for u in range(4):
                sp.dma_start(ctx_t[:, u, :], ctx_in[u]).then_inc(ctx_loaded[u], 16)
            for e in range(NE):
                sp.dma_start(wd[:, e, :, :], (w_down[e] if e < E else sw_down).rearrange("(k p) c -> p k c", p=128))\
                    .then_inc(wd_in, 16)

            def turn_x2(b):
                if w.it is None and b + 4 >= B:
                    return
                w.bank_read(("turn_x2", b))
                sp.dma_start(ctx_t[:, b % 4, :], ctx_in[bass.ds(w.batch(b + 4), 1), :, :].rearrange("a t c -> t (a c)"))\
                    .then_inc(ctx_loaded[b % 4], 16)

            def stack_lo(b):
                w.ge(stacked, b + 1)
                w.alone()
                if b < 4:
                    sp.wait_ge(const_ready, CONSTS + STORES)
                    sp.wait_ge(q_cleared, 1)
                w.ge(scored, NJ * (b - 1), NJ)
                for i in range(HJ):
                    r = slice(HR * i, HR * (i + 1))
                    sp.dma_start(k_slots[r, b % 2, :, i, :].bitcast(fp32), qk_stack[r, b % 4, NJ:, :].bitcast(fp32)).then_inc(k_slotted[b % 4], 16)
                w.ge(scored_t, NJ * (b - 3), NJ)
                for i in range(HJ):
                    r = slice(HR * i, HR * (i + 1))
                    sp.dma_start(q_slots[r, b % 4, :, i, :].bitcast(fp32), qk_stack[r, b % 4, 0:NJ, :].bitcast(fp32)).then_inc(q_slotted[b % 4], 16)

            def turn_max(b):
                w.bank_read(("turn_max", b))
                w.alone()
                if b < 4:
                    sp.wait_ge(q_cleared, 1)
                w.ge(scored_t, NJ * (b - 3), NJ)
                w.alone()
                sp.dma_start(q_slots[KR:KR + 1, b % 4].rearrange("p j i t -> p (j i) t").bitcast(fp32), max_rows[:].bitcast(fp32))\
                    .then_inc(max_placed, 16)

            w.run(dict(turn_x2=turn_x2, stack_lo=stack_lo, turn_max=turn_max))
            sp.wait_ge(stacked, B)
            sp.wait_ge(rounded, B)
            w.bank_read(("project_v", B - 1))
            for e in range(NE):
                for k, m in enumerate((w_gate[e], w_up[e]) if e < E else (sw_gate, sw_up)):
                    dst = t_qk[:, e, :] if e < E else xT[:]
                    sp.dma_start(dst[:, k * FF:(k + 1) * FF], m).then_inc(wgu_in, 16)
            with sp.Fori(0, NG) as g:
                sp.wait_ge(mixed, g * NE + NE)
                sp.dma_start(out[bass.ds(g * GB, GB), :, :].rearrange("b t c -> t b c"),
                             res[:, bass.ds(g * GB, GB), :]).then_inc(out_written, 16)
            sp.wait_ge(out_written, 16 * NG)

        @block.gpsimd
        def _(pool):
            w = Waits(pool)
            steps = [0]

            def step(ins):
                steps[0] += 1
                ins.then_inc(pool_step, 1)
                pool.wait_ge(pool_step, steps[0])

            def const(ins):
                consts[0] += 1
                ins.then_inc(const_ready, 1)
                pool.wait_ge(const_ready, consts[0])

            consts = [0]
            for m in (ident, ident16):
                const(pool.memset(m[:], 0.0))
                const(pool.affine_select(out=m[:], in_=m[:], compare_op=ALU.not_equal, fill=1.0, base=0,
                                         pattern=[[-1, 128]], channel_multiplier=1))
            const(pool.memset(causal[:], 0.0))
            const(pool.affine_select(out=causal[:], in_=causal[:], compare_op=ALU.is_ge, fill=MASKED, base=0,
                                     pattern=[[0, HJ], [-1, T]], channel_multiplier=1))
            const(pool.memset(eps[:], EPS))
            const(pool.memset(one_row[:], 1.0))
            const(pool.memset(k_slots[:].bitcast(fp32), 0.0))
            const(pool.memset(vst[:], 0.0))
            const(pool.memset(vst[:, :, :, HD:HD + 1], 1.0))
            assert consts[0] == CONSTS + STORES

            def norm_x(g):
                w.ge_group(x_rstd, g + 1)
                w.bank_read(("turn_x", g - 1))
                w.alone()
                part = res[:, bass.ds(w.batch(g * GB), GB), :]
                pool.tensor_tensor(xn1[:], part, mv1[:, :, 0:1].broadcast_to([T, GB, C]), ALU.subtract).then_inc(x_centred, 1)
                w.ge_group(x_centred, g + 1)
                w.alone()
                pool.tensor_tensor(xn1[:], xn1[:], rs1[:].rearrange("p (u a) -> p u a", a=1).broadcast_to([T, GB, C]), ALU.mult)\
                    .then_inc(x_normed, 1)
                w.ge_group(x_normed, g + 1)
                if g == 0:
                    pool.wait_ge(setup_done, 1)
                w.alone()
                pool.tensor_tensor(part, part, bias1[:].rearrange("p (a c) -> p a c", a=1).broadcast_to([T, GB, C]), ALU.add)\
                    .then_inc(xbias_added, 1)

            def norm_xattn(b):
                w.ge(x1_rstd, b + 1)
                w.bank_read(("turn_x2", b - 1))
                w.alone()
                pool.tensor_scalar(xn2[:], x1[:, b % 4, :], mv2[:, 0:1], rs2[:, 0:1], ALU.subtract, ALU.mult)\
                    .then_inc(xn2_ready, 1)

            def norm_ffn(b):
                w.ge(x2_rstd, b + 1)
                w.bank_read(("turn_ffn", b - 1))
                w.alone()
                pool.tensor_tensor(xn3[:], res[:, bass.ds(w.batch(b), 1), :].rearrange("p a c -> p (a c)"),
                                   mv3[:, 0:1].broadcast_to([T, C]), ALU.subtract).then_inc(x2_centred, 1)
                w.ge(x2_centred, b + 1)
                w.alone()
                pool.tensor_tensor(xn3[:], xn3[:], rs3[:, 0:1].broadcast_to([T, C]), ALU.mult).then_inc(xn3_ready, 1)

            def scores_t(b, j):
                w.ge(exped, NJ * b + j + 1, NJ)
                w.alone()
                part = probs[:, b % 2, j * HJ:(j + 1) * HJ, :]
                pool.affine_select(out=part, in_=part, compare_op=ALU.is_ge, fill=0.0, base=0,
                                   pattern=[[0, HJ], [1, T]], channel_multiplier=-1).then_inc(probs_ready, 1)

            def attn_out(b):
                w.bank_read(("attn_out", b))
                w.bank_read(("xout", b - 4))
                pool.tensor_tensor(x1b[:, b % 4, :], x1[:, b % 4, :], bias2[:], ALU.add).then_inc(x1b_ready, 1)

            w.run({"norm_x": norm_x, "norm_xattn": norm_xattn, "norm_ffn": norm_ffn, "scores_t": scores_t,
                   "attn_out": attn_out})

            pool.wait_ge(wgu_in, 16 * 2 * NE)
            pool.wait_ge(scored_t, NJ * B)
            for e in range(NE):
                raw = t_qk[:, e, :] if e < E else xT[:]
                step(pool.tensor_scalar(wgu_hi[:, e, :], raw, 1.0, None, ALU.mult))
                pool.tensor_tensor(wgu_lo[:, e, :], raw, wgu_hi[:, e, :].bitcast(fp32), ALU.subtract).then_inc(wgu_split, 1)

        @block.tensor
        def _(pe):
            w = Waits(pe)
            pe.wait_ge(const_ready, CONSTS)
            pe.wait_ge(w_in, 16 * W_LOADS)
            pe.wait_ge(dve_step, 1)
            for k in range(3):
                pe.transpose(PM[0][:, k * C:(k + 1) * C], wa[:, k, :], ident[:])
            pe.transpose(PM[0][:, 3 * C:4 * C], wsq[:, 0, :], ident[:]).then_inc(filled[0], 1)
            pe.transpose(PM[1][:, 0:C], wsq[:, 4, :], ident[:])
            for k in range(2 * NJ):
                pe.matmul(PM[1][0:KR, 2 * C + k:2 * C + k + 1], brow[:, k, :], one_row[:, 0:1], start=True, stop=True)
            pe.transpose(PM[1][:, C:C + NE], wr[:], ident[0:NE, 0:NE]).then_inc(filled[1], 1)
            pe.matmul(PM[2][:, 0:C], wsq[:, 3, :], wsq[:, 1, :], start=True, stop=True)
            pe.matmul(PM[2][:, C:C + 1], wsq[:, 1, :], cols[:, 2:3], start=True, stop=True).then_inc(filled[2], 1)
            pe.wait_ge(drained[0], 1)
            pe.wait_ge(drained[1], 1)
            pe.matmul(PM[3][:, 0:C], wsq[:, 2, :], woT[:], start=True, stop=True)
            pe.matmul(PM[3][:, C:2 * C], bcol[:, 0, :], wpT[:], start=True, stop=False)
            pe.matmul(PM[3][:, C:2 * C], one_row[:], rows[:, 0, :], start=False, stop=True)
            pe.matmul(PM[3][:, 2 * C:3 * C], bcol[:, 1, :], woT[:], start=True, stop=False)
            pe.matmul(PM[3][:, 2 * C:3 * C], one_row[:], rows[:, 1, :], start=False, stop=True).then_inc(filled[3], 1)

            def turn_x(g):
                bank = w.bank_free(("turn_x", g))
                w.ge_group(x_normed, g + 1)
                for u in range(GB):
                    mm = pe.transpose(bank[:, u * T:(u + 1) * T], xn1[:, u, :], ident[:])
                mm.then_inc(put_bank(("turn_x", g)), 1)

            def project(g, n):
                col = (n + NJ) % (2 * NJ)
                bank = w.bank_free(("project", g, n))
                w.ge_group(xT_split, g + 1)
                if g == 0 and n == 0:
                    pe.wait_ge(setup_done, 1)
                parts = ((wqk_hi, xT_hi), (wqk_hi, xT_lo), (wqk_lo, xT_hi))
                for k, (a, m) in enumerate(parts):
                    mm = pe.matmul(bank[0:KR, :], a[:, col, :], m[:, 0, :], start=(k == 0), stop=(k == 2))
                mm.then_inc(put_bank(("project", g, n)), 1)

            def project_v(b):
                bank = w.bank_free(("project_v", b))
                w.ge_group(xT_split, b // GB + 1)
                if b < GB:
                    pe.wait_ge(setup_done, 1)
                pe.matmul(bank[:, 0:C], xT[:, (b % GB) * T:(b % GB + 1) * T], wvT[:], start=True, stop=True)\
                    .then_inc(put_bank(("project_v", b)), 1)

            def scores(b, j):
                n = NJ * b + j
                w.ge(maxed, n - 1, NJ)
                if j == 0:
                    pe.wait_ge(k_slotted[b % 4], w.count(16 * HJ * (b // 4 + 1), 16 * HJ))
                pe.matmul(PS[j % 2][:], ident16[:], causal[:].rearrange("p a t -> p (a t)"), start=True, stop=False)
                pe.matmul(PS[j % 2][:], qk_stack[0:KR, b % 4, j, :], k_slots[:, b % 2, j].rearrange("p a t -> p (a t)"), start=False, stop=True)\
                    .then_inc(scored, 1)

            def turn_max(b):
                bank = w.bank_free(("turn_max", b))
                w.ge(maxed, NJ * (b + 1), NJ)
                pe.transpose(bank[0:NH, 0:T], negmax[:, b % 2, :], ident[:]).then_inc(put_bank(("turn_max", b)), 1)

            def scores_t(b, j):
                n = NJ * b + j
                w.ge(exped, n - 1, NJ)
                if j == 0:
                    w.ge(max_placed, 16 * (b + 1), 16)
                    pe.wait_ge(q_slotted[b % 4], w.count(16 * HJ * (b // 4 + 1), 16 * HJ))
                pe.matmul(PT[j % 2][:], qk_stack[:, b % 4, NJ + j, :], q_slots[:, b % 4, j].rearrange("p a t -> p (a t)"),
                          start=True, stop=True).then_inc(scored_t, 1)

            def values(b):
                bank = w.bank_free(("values", b))
                w.ge(probs_ready, NJ * (b + 1), NJ)
                w.bank_read(("project_v", b))
                for j in range(NJ):
                    for i in range(HJ):
                        h = j * HJ + i
                        mm = pe.matmul(bank[VW * i:VW * (i + 1), j * T:(j + 1) * T], vst[:, b % 4, h, :],
                                       probs[:, b % 2, h, :], start=True, stop=True, skip_group_check=True)
                mm.then_inc(put_bank(("values", b)), 1)

            def tall_sums(b):
                bank = w.bank_free(("tall_sums", b))
                w.bank_read(("values", b))
                for j in range(NJ):
                    mm = pe.transpose(bank[:, j * T:(j + 1) * T], yu[:, j * T:(j + 1) * T], ident[:])
                mm.then_inc(put_bank(("tall_sums", b)), 1)

            def turn_y(b):
                bank = w.bank_free(("turn_y", b))
                w.bank_read(("tall_sums", b))
                pe.transpose(bank[:, 0:T], yn[:], ident[:]).then_inc(put_bank(("turn_y", b)), 1)

            def attn_out(b):
                bank = w.bank_free(("attn_out", b))
                w.bank_read(("turn_y", b))
                pe.matmul(bank[:, 0:C], ynT[:], wpT[:], start=True, stop=True).then_inc(put_bank(("attn_out", b)), 1)

            def turn_x2(b):
                bank = w.bank_free(("turn_x2", b))
                w.ge(xn2_ready, b + 1)
                pe.wait_ge(ctx_loaded[b % 4], w.count(16 * (b // 4 + 1), 16))
                pe.transpose(bank[:, 0:T], xn2[:], ident[:])
                pe.transpose(bank[:, T:2 * T], ctx_t[:, b % 4, :], ident[:])\
                    .then_inc(put_bank(("turn_x2", b)), 1)

            def xproject(b):
                bank = w.bank_free(("xproject", b))
                w.bank_read(("turn_x2", b))
                pe.matmul(bank[:, 0:T], wA[:], xcT[:, b % 2, 0, :], start=True, stop=True)
                pe.matmul(bank[:, T:2 * T], xcT[:, b % 2, 1, :], wM[:], start=True, stop=True)\
                    .then_inc(put_bank(("xproject", b)), 1)

            def xscores(b):
                bank = w.bank_free(("xscores", b))
                w.bank_read(("xproject", b))
                pe.matmul(bank[:, 0:T], qa[:], xcT[:, b % 2, 1, :], start=True, stop=True)\
                    .then_inc(put_bank(("xscores", b)), 1)

            def turn_xprobs(b):
                bank = w.bank_free(("turn_xprobs", b))
                w.bank_read(("xscores", b))
                pe.transpose(bank[:, 0:T], xprobs[:], ident[:]).then_inc(put_bank(("turn_xprobs", b)), 1)

            def xout(b):
                bank = w.bank_free(("xout", b))
                w.bank_read(("turn_xprobs", b))
                pe.matmul(bank[:, 0:C], xprobsT[:], cm[:, b % 2, :], start=True, stop=True)\
                    .then_inc(put_bank(("xout", b)), 1)

            def turn_ffn(b):
                bank = w.bank_free(("turn_ffn", b))
                w.ge(xn3_ready, b + 1)
                pe.transpose(bank[:, 0:T], xn3[:], ident[:]).then_inc(put_bank(("turn_ffn", b)), 1)

            def router(b):
                bank = w.bank_free(("router", b))
                w.bank_read(("turn_ffn", b))
                pe.matmul(bank[:, 0:NE], x3s[:], wrT[:], start=True, stop=True).then_inc(put_bank(("router", b)), 1)

            w.run(dict(turn_x=turn_x, project=project, project_v=project_v, scores=scores, turn_max=turn_max, scores_t=scores_t,
                       values=values, tall_sums=tall_sums, turn_y=turn_y, attn_out=attn_out, turn_x2=turn_x2,
                       xproject=xproject, xscores=xscores, turn_xprobs=turn_xprobs, xout=xout, turn_ffn=turn_ffn,
                       router=router))

            pe.wait_ge(maxed, NJ * B)
            pe.wait_ge(exped, NJ * B)

            def gate_up(n, base, g2):
                e, k = n % NE, n // NE
                if e == 0:
                    pe.wait_ge(xb_split, g2 * 2 + k + 1)
                if base is None and k == 0:
                    pe.wait_ge(wgu_split, e + 1)
                for f in range(FT):
                    if not (n == 0 and base is None):
                        pe.wait_ge(h_ready, FT * n + f - FT + 1 if base is None else base * FT + (FT * n + f - FT + 1))
                    for dst, col, done in ((PS[f], f * 128, gate_done), (PT[f], FF + f * 128, up_done)):
                        for r, (a, m) in enumerate(((wgu_hi, xT_hi), (wgu_hi, xT_lo), (wgu_lo, xT_hi))):
                            mm = pe.matmul(dst[:], a[:, e, col:col + 128], m[:, k, :], start=(r == 0), stop=(r == 2))
                        mm.then_inc(done, 1)

            def down(n, base):
                e = n % NE
                pe.wait_ge(h_ready, FT * (n + 1) if base is None else base * FT + FT * (n + 1))
                if base is None and n == 0:
                    pe.wait_ge(wd_in, 16 * NE)
                    for k in range(2):
                        pe.wait_ge(drained[k], FILLS[k])
                if not (n < 2 and base is None):
                    pe.wait_ge(mixed, n - 1 if base is None else base + (n - 1))
                for f in range(FT):
                    for t in range(GB):
                        mm = pe.matmul(PM[n % 2][:, t * C:(t + 1) * C], h_all[:, n % 2, f, t * T:(t + 1) * T],
                                       wd[:, e, f, :], start=(f == 0 and t == 0), stop=(f == FT - 1 and t == GB - 1),
                                       skip_group_check=True)
                mm.then_inc(down_done, 1)

            def pair(g2, base):
                for n in range(2 * NE):
                    gate_up(n, base, g2)
                    if n:
                        down(n - 1, base)
                down(2 * NE - 1, base)

            pair(0, None)
            with pe.Fori(1, NG // 2) as g2:
                pair(g2, g2 * (2 * NE))

        @block.scalar
        def _(act):
            w = Waits(act)
            act.preload_act_table_set("natural_log_exp_and_others")

            def turn_max(b):
                bank, drain = w.bank_filled(("turn_max", b))
                w.ge(max_placed, 16 * b, 16)
                act.activation(max_rows[:], bank[0:NH, 0:T], ACT.Copy).then_inc(drain, 1)

            def rstd_x(g):
                w.ge_group(x_stats, g + 1)
                if g == 0:
                    act.wait_ge(const_ready, CONSTS)
                act.activation(ln1[:], mv1[:, :, 1], ACT.Ln, bias=eps[:, 0:1]).then_inc(x_ln, 1)
                w.ge_group(x_ln, g + 1)
                act.activation(rs1[:], ln1[:], ACT.Exp, scale=-0.5).then_inc(x_rstd, 1)

            def turn_x(g):
                bank, drain = w.bank_filled(("turn_x", g))
                act.activation(xT_hi[:, 0, :], bank[:], ACT.Copy).then_inc(xhi_done, 1)
                act.activation(xT[:], bank[:], ACT.Copy).then_inc(drain, 1)

            def stacks(b):
                u = b % GB
                w.bank_read(("project", b // GB, 7))
                w.ge(scored_t, NJ * (b - 3), NJ)
                act.activation(qk_stack[0:KR, b % 4], t_qk[0:KR, :, u * T:(u + 1) * T], ACT.Copy).then_inc(rounded, 1)

            def project_v(b):
                bank, drain = w.bank_filled(("project_v", b))
                if b < GB:
                    act.wait_ge(const_ready, CONSTS + STORES)
                act.activation(vst[:, b % 4, :, 0:HD], bank[:, 0:C].rearrange("p (h d) -> p h d", d=HD), ACT.Copy)\
                    .then_inc(drain, 1)

            def scores_t(b, j):
                w.ge(scored_t, NJ * b + j + 1, NJ)
                act.activation(probs[:, b % 2, j * HJ:(j + 1) * HJ, :].rearrange("p a t -> p (a t)"), PT[j % 2][:], ACT.Exp)\
                    .then_inc(exped, 1)

            def values(b):
                bank, drain = w.bank_filled(("values", b))
                w.bank_read(("tall_sums", b - 1))
                act.activation(yu[:], bank[:], ACT.Copy).then_inc(drain, 1)

            def turn_y(b):
                bank, drain = w.bank_filled(("turn_y", b))
                w.bank_read(("attn_out", b - 1))
                act.activation(ynT[:], bank[:, 0:T], ACT.Copy).then_inc(drain, 1)

            def rstd_xattn(b):
                w.ge(x1_stats, b + 1)
                act.activation(ln2[:], mv2[:, 1:2], ACT.Ln, bias=eps[:, 0:1]).then_inc(x1_ln, 1)
                w.ge(x1_ln, b + 1)
                act.activation(rs2[:], ln2[:], ACT.Exp, scale=-0.5).then_inc(x1_rstd, 1)

            def turn_x2(b):
                bank, drain = w.bank_filled(("turn_x2", b))
                act.activation(xcT[:, b % 2].rearrange("p a t -> p (a t)"), bank[:, 0:2 * T], ACT.Copy).then_inc(drain, 1)

            def xproject(b):
                bank, drain = w.bank_filled(("xproject", b))
                w.bank_read(("xout", b - 2))
                act.activation(qa[:], bank[:, 0:T], ACT.Identity, bias=bqA[:, 0:1])
                act.activation(cm[:, b % 2, :], bank[:, T:2 * T], ACT.Copy).then_inc(drain, 1)

            def xscores(b):
                bank, drain = w.bank_filled(("xscores", b))
                w.ge(xneg_ready, b + 1)
                w.bank_read(("turn_xprobs", b - 1))
                w.ge(x_inverse, b - 1)
                act.activation(xprobs[:], bank[:, 0:T], ACT.Exp, bias=xneg[:, 0:1], accum_out=xsum[:, b % 2, :]).then_inc(drain, 1)

            def turn_xprobs(b):
                bank, drain = w.bank_filled(("turn_xprobs", b))
                w.bank_read(("xout", b - 1))
                act.activation(xprobsT[:], bank[:, 0:T], ACT.Copy).then_inc(drain, 1)

            def rstd_ffn(b):
                w.ge(x2_stats, b + 1)
                act.activation(ln3[:], mv3[:, 1:2], ACT.Ln, bias=eps[:, 0:1]).then_inc(x2_ln, 1)
                w.ge(x2_ln, b + 1)
                act.activation(rs3[:], ln3[:], ACT.Exp, scale=-0.5).then_inc(x2_rstd, 1)

            def turn_ffn(b):
                bank, drain = w.bank_filled(("turn_ffn", b))
                w.bank_read(("router", b - 1))
                act.activation(x3T[:, bass.ds(w.batch(b) * T, T)], bank[:, 0:T], ACT.Copy)
                act.activation(x3s[:], bank[:, 0:T], ACT.Copy).then_inc(drain, 1)

            w.run(dict(turn_max=turn_max, rstd_x=rstd_x, turn_x=turn_x, stacks=stacks, project_v=project_v,
                       scores_t=scores_t, values=values, turn_y=turn_y, rstd_xattn=rstd_xattn, turn_x2=turn_x2,
                       xproject=xproject, xscores=xscores, turn_xprobs=turn_xprobs, rstd_ffn=rstd_ffn, turn_ffn=turn_ffn))

            act.wait_ge(centred, 1)
            act.activation(cw[:], cw[:], ACT.Exp).then_inc(route_exped, 1)

            def group(base):
                for n in range(2 * NE):
                    for f in range(FT):
                        m = FT * n + f
                        act.wait_ge(gate_done, m + 1 if base is None else base * FT + (m + 1))
                        if not (n == 0 and base is None):
                            act.wait_ge(h_ready, m - FT + 1 if base is None else base * FT + (m - FT + 1))
                        act.activation(silu[:, f, :], PS[f][:], ACT.Silu).then_inc(silu_done, 1)

            group(None)
            with act.Fori(1, NG // 2) as g2:
                group(g2 * (2 * NE))

        @block.vector
        def _(dve):
            w = Waits(dve)
            steps = [0]

            def step(ins):
                steps[0] += 1
                ins.then_inc(dve_step, 1)
                dve.wait_ge(dve_step, steps[0])

            def group_stats(g):
                if g == 0:
                    dve.wait_ge(x_in[0], 16)
                elif g == 1:
                    dve.wait_ge(x_in[1], 16)
                for u in range(GB):
                    ins = dve.bn_stats(st1[:, u, :], res[:, bass.ds(w.batch(g * GB + u), 1), :].rearrange("p a c -> p (a c)"))
                ins.then_inc(x_part, 1)
                w.ge_group(x_part, g + 1)
                w.alone()
                w.ge_group(x_normed, g)
                w.alone()
                for u in range(GB):
                    ins = dve.bn_aggr(mv1[:, u, :], st1[:, u, :])
                ins.then_inc(x_stats, 1)

            group_stats(0)
            dve.memset(qk_stack[KR:KR + 1, :, NJ:, :].bitcast(fp32), 1.0)
            dve.memset(q_slots.bitcast(fp32), 0.0).then_inc(q_cleared, 1)
            dve.wait_ge(w_in, 16 * W_LOADS)
            dve.tensor_copy(brow.rearrange("p k (i a d) -> p (k i) a d", i=HJ, a=3),
                            rows[:, 2:4, :].rearrange("p k (i a d) -> p (k i) a d", a=1, d=HD).broadcast_to([1, 2 * NH, 3, HD]))
            step(dve.tensor_copy(bcol, cols[:, 0:2].rearrange("p (k a) -> p k a", a=1).broadcast_to([C, 2, C])))
            dve.wait_ge(filled[1], 1)
            dve.tensor_copy(bqk[:], PM[1][0:KR, 2 * C:2 * C + 2 * NJ])
            dve.tensor_copy(woT[:], PM[1][:, 0:C])
            dve.tensor_copy(wrT[:], PM[1][:, C:C + NE]).then_inc(drained[1], 1)
            dve.wait_ge(filled[0], 1)
            dve.tensor_copy(wqkT.rearrange("p k c -> p (k c)"), PM[0][:, 0:2 * C])
            dve.tensor_copy(wvT[:], PM[0][:, 2 * C:3 * C])
            dve.tensor_copy(wpT[:], PM[0][:, 3 * C:4 * C]).then_inc(drained[0], 1)
            dve.wait_ge(drained[0], 1)
            wqk = wqkT.rearrange("p k (i a d) -> p (k i) a d", a=1, d=HD).broadcast_to([C, 2 * NH, 3, HD])
            hi, lo = (m[:].rearrange("p k (i a d) -> p (k i) a d", i=HJ, a=3) for m in (wqk_hi, wqk_lo))
            step(dve.tensor_copy(hi, wqk))
            dve.tensor_tensor(lo, wqk, hi.bitcast(fp32), ALU.subtract)
            dve.wait_ge(filled[2], 1)
            dve.tensor_scalar(wA[:], PM[2][:, 0:C], XSCALE, None, ALU.mult)
            dve.tensor_scalar(bqA[:], PM[2][:, C:C + 1], XSCALE, None, ALU.mult).then_inc(drained[2], 1)
            dve.wait_ge(filled[3], 1)
            dve.tensor_copy(wM[:], PM[3][:, 0:C])
            dve.tensor_copy(bias1[:], PM[3][:, C:2 * C])
            dve.tensor_copy(bias2[:], PM[3][:, 2 * C:3 * C]).then_inc(drained[3], 1)
            dve.wait_ge(drained[3], 1)
            dve.memset(gexp[:], 0.0).then_inc(setup_done, 1)

            def norm_x_stats(g):
                if g > 0:
                    group_stats(g)

            def turn_x(g):
                w.bank_read(("turn_x", g))
                w.ge_group(xhi_done, g + 1)
                dve.tensor_tensor(xT_lo[:, 0, :], xT[:], xT_hi[:, 0, :].bitcast(fp32), ALU.subtract).then_inc(xT_split, 1)

            def project(g, n):
                bank, drain = w.bank_filled(("project", g, n))
                col = (n + NJ) % (2 * NJ)
                w.ge(stacked, g * GB)
                dve.scalar_tensor_tensor(out=t_qk[0:KR, col, :].rearrange("p (u t) -> p u t", u=GB),
                                         in0=bank[0:KR, :].rearrange("p (u t) -> p u t", u=GB), scalar=bqk[:, col:col + 1],
                                         in1=ropes[:, col // NJ, :].rearrange("p (a t) -> p a t", a=1).broadcast_to([KR, GB, T]),
                                         op0=ALU.add, op1=ALU.mult).then_inc(drain, 1)

            def stack_lo(b):
                u = b % GB
                w.ge(rounded, b + 1)
                for k, cs in enumerate((slice(0, NJ), slice(NJ, 2 * NJ))):
                    part = qk_stack[0:KR, b % 4, cs, :]
                    ins = dve.scalar_tensor_tensor(out=part, in0=part.bitcast(fp32), scalar=lo_rows[:, k:k + 1],
                                                   in1=t_qk[0:KR, cs, u * T:(u + 1) * T], op0=ALU.mult, op1=ALU.add)
                ins.then_inc(stacked, 1)

            def scores(b, j):
                w.ge(scored, NJ * b + j + 1, NJ)
                if j == 0:
                    w.bank_read(("turn_max", b - 2))
                dve.reduce_max(negmax[:, b % 2, j * HJ:(j + 1) * HJ], PS[j % 2][:].rearrange("p (i t) -> p i t", i=HJ),
                               axis=AX.X, negate=True).then_inc(maxed, 1)

            def tall_sums(b):
                bank, drain = w.bank_filled(("tall_sums", b))
                heads = bank[:].rearrange("p (h v) -> p h v", v=VW)
                dve.reciprocal(ysum[:].rearrange("p (h a) -> p h a", a=1), heads[:, :, HD:HD + 1]).then_inc(y_inverse, 1)
                w.ge(y_inverse, b + 1)
                w.bank_read(("turn_y", b - 1))
                dve.tensor_tensor(yn[:].rearrange("p (h d) -> p h d", d=HD), heads[:, :, 0:HD],
                                  ysum[:].rearrange("p (h a) -> p h a", a=1).broadcast_to([T, NH, HD]), ALU.mult)\
                    .then_inc(drain, 1)

            def one(b):
                return res[:, bass.ds(w.batch(b), 1), :].rearrange("p a c -> p (a c)")

            def attn_out(b):
                bank, drain = w.bank_filled(("attn_out", b))
                w.ge_group(xbias_added, b // GB + 1)
                w.ge(x1b_ready, b - 3)
                w.ge(xn2_ready, b - 3)
                dve.tensor_tensor(x1[:, b % 4, :], bank[:, 0:C], one(b), ALU.add).then_inc(drain, 1)
                w.bank_read(("attn_out", b))
                w.alone()
                dve.bn_stats(st2[:], x1[:, b % 4, :]).then_inc(x1_part, 1)
                w.ge(x1_part, b + 1)
                w.ge(xn2_ready, b)
                w.alone()
                dve.bn_aggr(mv2[:], st2[:]).then_inc(x1_stats, 1)

            def xscores(b):
                bank, _ = w.bank_filled(("xscores", b))
                w.bank_read(("xscores", b - 1))
                dve.reduce_max(xneg[:], bank[:, 0:T], axis=AX.X, negate=True).then_inc(xneg_ready, 1)

            def turn_xprobs(b):
                w.bank_read(("xscores", b))
                dve.reciprocal(xinv[:], xsum[:, b % 2, :]).then_inc(x_inverse, 1)

            def xout(b):
                bank, drain = w.bank_filled(("xout", b))
                w.ge(x_inverse, b + 1)
                w.ge(x1b_ready, b + 1)
                dve.scalar_tensor_tensor(out=one(b), in0=bank[:, 0:C], scalar=xinv[:, 0:1], in1=x1b[:, b % 4, :],
                                         op0=ALU.mult, op1=ALU.add).then_inc(drain, 1)
                w.bank_read(("xout", b))
                w.alone()
                dve.bn_stats(st3[:], one(b)).then_inc(x2_part, 1)
                w.ge(x2_part, b + 1)
                w.ge(xn3_ready, b)
                w.alone()
                dve.bn_aggr(mv3[:], st3[:]).then_inc(x2_stats, 1)

            def router(b):
                bank, drain = w.bank_filled(("router", b))
                dve.tensor_copy(logit[:, bass.ds(w.batch(b), 1), :].rearrange("p a e -> p (a e)"), bank[:, 0:NE])\
                    .then_inc(drain, 1)

            w.run(dict(norm_x_stats=norm_x_stats, turn_x=turn_x, project=project, stack_lo=stack_lo,
                       scores=scores, tall_sums=tall_sums, attn_out=attn_out, xscores=xscores,
                       turn_xprobs=turn_xprobs, xout=xout, router=router))

            def split(g, k):
                src = x3T[:, bass.ds(g * (GB * T), GB * T)]
                dve.tensor_copy(xT_hi[:, k, :], src).then_inc(xb_hi_done, 1)
                dve.wait_ge(xb_hi_done, g + 1)
                dve.tensor_tensor(xT_lo[:, k, :], src, xT_hi[:, k, :].bitcast(fp32), ALU.subtract).then_inc(xb_split, 1)

            last = FILL[("router", B - 1)]
            dve.wait_ge(drained[last[0]], last[1] + 1)
            split(0, 0)
            lg, ex = logit[:, :, 0:E], cw[:, :, 0:E]
            for e in range(E):
                ins = dve.memset(ramp[:, :, e:e + 1], float(E - e))
            step(ins)
            step(dve.reduce_max(top_p[:].rearrange("p b a -> p (b a)"), lg, axis=AX.X))
            step(dve.tensor_tensor(ex, lg, top_p[:].broadcast_to([T, B, E]), ALU.subtract))
            dve.tensor_scalar(cw[:, :, E:NE], logit[:, :, E:NE], -1.0, None, ALU.mult).then_inc(centred, 1)

            def route():
                dve.wait_ge(route_exped, 1)
                step(dve.reduce_sum(top_p[:].rearrange("p b a -> p (b a)"), ex, axis=AX.X))
                step(dve.reciprocal(gexp[:], top_p[:]))
                step(dve.tensor_tensor(pick, ex, gexp[:].broadcast_to([T, B, E]), ALU.mult))
                left = pick
                for k, sel in enumerate((sel1, sel2)):
                    step(dve.reduce_max(top_p[:].rearrange("p b a -> p (b a)"), left, axis=AX.X))
                    step(dve.tensor_tensor(sel, left, top_p[:].broadcast_to([T, B, E]), ALU.is_ge))
                    step(dve.tensor_tensor(sel, sel, ramp, ALU.mult))
                    step(dve.reduce_max(top_p[:].rearrange("p b a -> p (b a)"), sel, axis=AX.X))
                    step(dve.tensor_tensor(sel, ramp, top_p[:].broadcast_to([T, B, E]), ALU.is_equal))
                    if k == 0:
                        step(dve.scalar_tensor_tensor(out=rest, in0=sel1, scalar=-2.0, in1=pick, op0=ALU.mult, op1=ALU.add))
                        left = rest
                step(dve.tensor_tensor(sel1, sel1, sel2, ALU.add))
                step(dve.tensor_tensor(ex, sel1, pick, ALU.mult))
                step(dve.tensor_scalar(gexp[:], cw[:, :, E:NE], 1.0, None, ALU.add))
                step(dve.reciprocal(cw[:, :, E:NE], gexp[:]))

            def group(g2, base, last_pair=False):
                for n in range(2 * NE):
                    e, k = n % NE, n // NE
                    g = g2 * 2 + k
                    if e == NE // 2 and not (last_pair and k == 1):
                        split(g + 1, 1 - k)
                    for f in range(FT):
                        m = FT * n + f + 1
                        dve.wait_ge(silu_done, m if base is None else base * FT + m)
                        dve.wait_ge(up_done, m if base is None else base * FT + m)
                        if not (n < 2 and base is None):
                            dve.wait_ge(down_done, n - 1 if base is None else base + (n - 1))
                        dve.tensor_tensor(h_all[:, n % 2, f, :], silu[:, f, :], PT[f][:], ALU.mult).then_inc(h_ready, 1)
                    if n == 1 and base is None:
                        route()
                    if n:
                        mix(g2, base, n - 1)
                mix(g2, base, 2 * NE - 1)

            def mix(g2, base, n):
                e, g = n % NE, g2 * 2 + n // NE
                dve.wait_ge(down_done, n + 1 if base is None else base + (n + 1))
                if not (n == 0 and base is None):
                    dve.wait_ge(mixed, n if base is None else base + n)
                for t in range(GB):
                    part = res[:, bass.ds(g * GB + t, 1), :].rearrange("p a c -> p (a c)")
                    ins = dve.scalar_tensor_tensor(out=part, in0=PM[n % 2][:, t * C:(t + 1) * C],
                                                   scalar=cw[:, bass.ds(g * GB + t, 1), e:e + 1].rearrange("p a e -> p (a e)"),
                                                   in1=part, op0=ALU.mult, op1=ALU.add)
                ins.then_inc(mixed, 1)

            group(0, None)
            with dve.Fori(1, NG // 2 - 1) as g2:
                group(g2, g2 * (2 * NE))
            group(NG // 2 - 1, (NG // 2 - 1) * 2 * NE, last_pair=True)


NAMES = ['x', 'ctx_1024', 'L0_attn_W_attn', 'L0_attn_b_attn', 'L0_attn_W_proj', 'L0_attn_b_proj', 'L0_xattn_Wk',
         'L0_xattn_Wv', 'L0_xattn_bv', 'L0_xattn_Wq', 'L0_xattn_bq', 'L0_xattn_Wo', 'L0_xattn_bo', 'L0_ffn_router_w',
         'L0_ffn_w_gate', 'L0_ffn_w_up', 'L0_ffn_w_down', 'L0_ffn_sw_gate', 'L0_ffn_sw_up', 'L0_ffn_sw_down',
         'L0_ffn_gate_w']


def lo_signs():
    import numpy as np
    term = np.arange(KR) // HD % 3
    return -np.stack([term == 2, term == 1], axis=1).astype(np.float32)


def rotary_factors():
    import numpy as np
    theta = (1.0 / np.float32(10000.0) ** (np.float32(2.0) * np.arange(HD // 2, dtype=np.float32) / HD)).astype(np.float32)
    ang = (np.arange(1, T + 1, dtype=np.float32)[None, :] * theta[:, None]).astype(np.float32)
    f = (np.cos(ang) + np.sin(ang)).astype(np.float32)
    f = f[np.arange(KR) % (HD // 2)]
    return np.stack([f * np.float32(QSCALE), f], axis=1).astype(np.float32)


def kernel(**inputs):
    import numpy as np
    import concourse.bacc as bacc
    from concourse.bass_utils import run_bass_kernel_spmd

    nc = bacc.Bacc("TRN2", target_bir_lowering=False, num_devices=1)
    arrays, args = {}, []
    for name, a in [(n, np.ascontiguousarray(inputs[n])) for n in NAMES] \
            + [("rotary", rotary_factors()), ("lo_signs", lo_signs())]:
        arrays[f"in_{name}"] = a
        args.append(nc.dram_tensor(f"in_{name}", a.shape, mybir.dt.from_np(a.dtype), kind="ExternalInput").ap())
    args.append(nc.dram_tensor("out_x", (B, T, C), fp32, kind="ExternalOutput").ap())
    build(nc, *args)
    return run_bass_kernel_spmd(nc, [arrays], core_ids=[0]).results[0]["out_x"]
```
